# Optimizing a Trainium2 kernel written in Bass

```python
import numpy as np
import jax
import jax.numpy as jnp

def _softmax(x, axis=-1):
    return jax.nn.softmax(x, axis=axis)

def _gelu(x):
    return jax.nn.gelu(x, approximate=True)

def _silu(x):
    return jax.nn.silu(x)

def _sigmoid(x):
    return jax.nn.sigmoid(x)

def _layernorm(x, axis=-1, eps=1e-05):
    m = jnp.mean(x, axis=axis, keepdims=True)
    v = jnp.var(x, axis=axis, keepdims=True)
    return (x - m) / jnp.sqrt(v + eps)

def _scatter_add(tgt, idx, src, axis=0):
    return tgt.at[idx].add(src)

def _segment_sum(src, seg, n):
    return jax.ops.segment_sum(src, seg, n)
kernel_name = 'mk_seq_postln_d1_jaxref_r8_0a2040'

def setup_inputs(seed: int=0):
    np.random.seed(seed)
    _w = jnp.asarray

    def _L0_attn_setup():
        import jax, jax.numpy as jnp
        import numpy as np
        N_HEAD = 16
        PAGE_SIZE = 32
        ROPE_THETA = 10000.0

        def _rope_tables(T, D, dtype):
            inv = 1.0 / ROPE_THETA ** (np.arange(0, D, 2, dtype=np.float32) / D)
            ang = np.outer(np.arange(T, dtype=np.float32), inv)
            return (jnp.asarray(np.cos(ang), dtype), jnp.asarray(np.sin(ang), dtype))

        def _apply_rope(x, cos, sin):
            x1 = x[..., 0::2]
            x2 = x[..., 1::2]
            c = cos[None, :, None, :]
            s = sin[None, :, None, :]
            out = jnp.stack([x1 * c - x2 * s, x1 * s + x2 * c], axis=-1)
            return out.reshape(x.shape)
        key = jax.random.key(seed)
        ks = jax.random.split(key, 6)
        B, T, E = (2, 256, 128)
        L = E // 2
        sc = lambda fan: 1.0 / np.sqrt(fan)
        return {'x': jax.random.normal(ks[0], (B, T, E), jnp.float32), 'wq': jax.random.normal(ks[1], (E, E), jnp.float32) * sc(E), 'w_down': jax.random.normal(ks[2], (E, L), jnp.float32) * sc(E), 'wk_up': jax.random.normal(ks[3], (L, E), jnp.float32) * sc(L), 'wv_up': jax.random.normal(ks[4], (L, E), jnp.float32) * sc(L), 'wo': jax.random.normal(ks[5], (E, E), jnp.float32) * sc(E)}
    _L0_attn_in = _L0_attn_setup()

    def _L0_ffn_setup():
        import jax, jax.numpy as jnp
        import numpy as np
        D, H, O, E, TOPK = (128, 512, 128, 8, 2)
        B, S = (4, 128)
        key = jax.random.key(seed)
        ks = jax.random.split(key, 12)
        std = 0.02
        return {'hidden_states': jax.random.normal(ks[0], (B, S, D), dtype=jnp.float32), 'norm_weight': jnp.ones((D,), dtype=jnp.float32), 'router_w': jax.random.normal(ks[1], (E, D), dtype=jnp.float32) * std, 'sw1': jax.random.normal(ks[2], (D, H), dtype=jnp.float32) * (1.0 / np.sqrt(D)), 'sb1': jnp.zeros((H,), dtype=jnp.float32), 'sw2': jax.random.normal(ks[3], (H, O), dtype=jnp.float32) * (1.0 / np.sqrt(H)), 'sb2': jnp.zeros((O,), dtype=jnp.float32), 'ew1': jax.random.normal(ks[4], (E, D, H), dtype=jnp.float32) * (1.0 / np.sqrt(D)), 'eb1': jnp.zeros((E, H), dtype=jnp.float32), 'ew2': jax.random.normal(ks[5], (E, H, O), dtype=jnp.float32) * (1.0 / np.sqrt(H)), 'eb2': jnp.zeros((E, O), dtype=jnp.float32)}
    _L0_ffn_in = _L0_ffn_setup()
    _d = {'L0_attn_x': _L0_attn_in['x'], 'L0_attn_wq': _L0_attn_in['wq'], 'L0_attn_w_down': _L0_attn_in['w_down'], 'L0_attn_wk_up': _L0_attn_in['wk_up'], 'L0_attn_wv_up': _L0_attn_in['wv_up'], 'L0_attn_wo': _L0_attn_in['wo'], 'L0_ffn_norm_weight': _L0_ffn_in['norm_weight'], 'L0_ffn_router_w': _L0_ffn_in['router_w'], 'L0_ffn_sw1': _L0_ffn_in['sw1'], 'L0_ffn_sb1': _L0_ffn_in['sb1'], 'L0_ffn_sw2': _L0_ffn_in['sw2'], 'L0_ffn_sb2': _L0_ffn_in['sb2'], 'L0_ffn_ew1': _L0_ffn_in['ew1'], 'L0_ffn_eb1': _L0_ffn_in['eb1'], 'L0_ffn_ew2': _L0_ffn_in['ew2'], 'L0_ffn_eb2': _L0_ffn_in['eb2']}
    _x0 = _d['L0_attn_x']
    _d['L0_attn_x'] = jax.random.normal(jax.random.fold_in(jax.random.key(seed), 1), (8, 512, 128), dtype=_x0.dtype)
    del _x0
    return _d

def reference(L0_attn_x, L0_attn_wq, L0_attn_w_down, L0_attn_wk_up, L0_attn_wv_up, L0_attn_wo, L0_ffn_norm_weight, L0_ffn_router_w, L0_ffn_sw1, L0_ffn_sb1, L0_ffn_sw2, L0_ffn_sb2, L0_ffn_ew1, L0_ffn_eb1, L0_ffn_ew2, L0_ffn_eb2):

    def _L0_attn_ref(x, wq, w_down, wk_up, wv_up, wo):
        import jax, jax.numpy as jnp
        import numpy as np
        N_HEAD = 16
        PAGE_SIZE = 32
        ROPE_THETA = 10000.0

        def _rope_tables(T, D, dtype):
            inv = 1.0 / ROPE_THETA ** (np.arange(0, D, 2, dtype=np.float32) / D)
            ang = np.outer(np.arange(T, dtype=np.float32), inv)
            return (jnp.asarray(np.cos(ang), dtype), jnp.asarray(np.sin(ang), dtype))

        def _apply_rope(x, cos, sin):
            x1 = x[..., 0::2]
            x2 = x[..., 1::2]
            c = cos[None, :, None, :]
            s = sin[None, :, None, :]
            out = jnp.stack([x1 * c - x2 * s, x1 * s + x2 * c], axis=-1)
            return out.reshape(x.shape)
        B, T, E = x.shape
        H = N_HEAD
        D = E // H
        q = (x @ wq).reshape(B, T, H, D)
        lat = x @ w_down
        k = (lat @ wk_up).reshape(B, T, H, D)
        v = (lat @ wv_up).reshape(B, T, H, D)
        cos, sin = _rope_tables(T, D, x.dtype)
        q = _apply_rope(q, cos, sin)
        k = _apply_rope(k, cos, sin)
        scale = 1.0 / jnp.sqrt(jnp.asarray(D, x.dtype))
        scores = jnp.einsum('bqhd,bkhd->bhqk', q, k) * scale
        pages = jnp.arange(T) // PAGE_SIZE
        allowed = pages[None, :] <= pages[:, None]
        scores = jnp.where(allowed[None, None], scores, jnp.finfo(scores.dtype).min)
        attn = jax.nn.softmax(scores, axis=-1)
        out = jnp.einsum('bhqk,bkhd->bqhd', attn, v).reshape(B, T, E)
        return out @ wo

    def _L0_ffn_ref(hidden_states, norm_weight, router_w, sw1, sb1, sw2, sb2, ew1, eb1, ew2, eb2):
        import jax, jax.numpy as jnp
        import numpy as np
        D, H, O, E, TOPK = (128, 512, 128, 8, 2)
        B, S = (4, 128)
        b, s, d = hidden_states.shape
        var = jnp.mean(jnp.square(hidden_states), axis=-1, keepdims=True)
        normed = hidden_states * jax.lax.rsqrt(var + 1e-08) * norm_weight
        shared = jnp.maximum(normed @ sw1 + sb1, 0.0) @ sw2 + sb2
        flat = normed.reshape(-1, d)
        T = flat.shape[0]
        probs = jax.nn.sigmoid(flat @ router_w.T)
        scores, idx = jax.lax.top_k(probs, TOPK)
        w = scores / (jnp.sum(scores, axis=-1, keepdims=True) + 1e-06)
        comb = jnp.zeros((T, E), dtype=flat.dtype)
        comb = comb.at[jnp.arange(T)[:, None], idx].add(w)
        h = jnp.maximum(jnp.einsum('td,edh->teh', flat, ew1) + eb1[None, :, :], 0.0)
        eo = jnp.einsum('teh,eho->teo', h, ew2) + eb2[None, :, :]
        routed = jnp.einsum('teo,te->to', eo, comb)
        return shared + routed.reshape(b, s, -1)
    x = L0_attn_x
    x = _layernorm(x + _L0_attn_ref(x, L0_attn_wq, L0_attn_w_down, L0_attn_wk_up, L0_attn_wv_up, L0_attn_wo), axis=-1)
    x = _layernorm(x + _L0_ffn_ref(x, L0_ffn_norm_weight, L0_ffn_router_w, L0_ffn_sw1, L0_ffn_sb1, L0_ffn_sw2, L0_ffn_sb2, L0_ffn_ew1, L0_ffn_eb1, L0_ffn_ew2, L0_ffn_eb2), axis=-1)
    return x

_drawn_inputs = setup_inputs


def setup_inputs(seed=0):
    import zlib

    import numpy as np

    out = dict(_drawn_inputs(seed))
    spreads = {'L0_ffn_norm_weight': (1.0, 0.2),
     'L0_ffn_sb1': (0.0, 0.1),
     'L0_ffn_sb2': (0.0, 0.1),
     'L0_ffn_eb1': (0.0, 0.1),
     'L0_ffn_eb2': (0.0, 0.1)}
    factors = {}
    for name, (base, spread) in spreads.items():
        noise = np.random.default_rng([zlib.crc32(name.encode()), seed]).standard_normal(out[name].shape)
        drawn = base * np.exp(spread * noise) if base else spread * noise
        out[name] = jnp.asarray(drawn.astype(out[name].dtype))
    for name, factor in factors.items():
        out[name] = (out[name] * factor).astype(out[name].dtype)
    return out
```

```python
from collections import deque
from contextlib import ExitStack

import numpy as np
import concourse.bass as bass
from concourse import mybir

F32 = mybir.dt.float32
BF16 = mybir.dt.bfloat16
U32 = mybir.dt.uint32
ACT = mybir.ActivationFunctionType
ALU = mybir.AluOpType
AXIS_X = mybir.AxisListType.X

P = 128
N_HEAD = 16
PAGE = 32
ROPE_THETA = 10000.0
TOPK = 2
LN_EPS = 1e-5
RMS_EPS = 1e-8
TOPK_EPS = 1e-6

HALF = 64
PARTS = 3
TERMS = [(0, 0), (0, 1), (1, 0), (1, 1), (0, 2), (2, 0)]
MASK_BIG = -1.0e38


class Lane:

    def __init__(self, engine, sem, serial=False):
        self.serial = serial
        self.engine, self.sem, self.count, self.seen = engine, sem, 0, {}

    def wait(self, tokens):
        for t in tokens:
            if t is None:
                continue
            sem, value = t
            if self.seen.get(sem.name, 0) < value:
                self.seen[sem.name] = value
                self.engine.wait_ge(sem, value)

    def do(self, make, after=(), signal=True):
        self.wait(after)
        if self.serial:
            self.wait([self.latest()])
        ins = make(self.engine)
        if not signal:
            return None
        self.count += 1
        ins.then_inc(self.sem, 1)
        return (self.sem, self.count)

    def latest(self):
        return (self.sem, self.count)

    def dma(self, out, src, counter, after=()):
        self.wait(after)
        counter.count += 16
        self.engine.dma_start(out, src).then_inc(counter.sem, 16)
        return (counter.sem, counter.count)


class Counter:

    def __init__(self, sem):
        self.sem, self.count = sem, 0

    def all(self):
        return (self.sem, self.count)


def build(nc, x, wq, w_down, wk_up, wv_up, wo, norm_weight, router_w, sw1, sb1, sw2, sb2,
          ew1, eb1, ew2, eb2, rope_cos, rope_sin, rope_swap, mask_rows, ident_in, ones_row_in,
          before_in, out):
    B, T, E = x.shape
    L = w_down.shape[1]
    D = E // N_HEAD
    NE, _, H = ew1.shape
    assert E == P and D == 8 and T == 512
    QT = T // P
    NT = B * QT
    HT = H // P
    NP = N_HEAD // 2
    GH = 4
    NG = N_HEAD // GH
    PPB = P // PAGE
    N_MASK = QT * (PPB - 1)
    ROW_TERM = PARTS
    ROW_MASK = ROW_TERM + D * len(TERMS)
    assert ROW_MASK + N_MASK <= HALF
    SCALE = 1.0 / float(np.sqrt(D))
    VW = 32
    SLOTS = 10
    LEAD = 6
    NSTACK = 3
    NPROB = 12

    ctx = ExitStack()
    with ctx:
        def sb(name, shape, dt=F32):
            return ctx.enter_context(nc.sbuf_tensor(name, shape, dt))

        def sem(name):
            return ctx.enter_context(nc.semaphore(name))

        psum = ctx.enter_context(nc.psum_tensor("psum", [P, 8, 512], F32))
        EXP_BANKS, MAX_BANKS, PV_BANK, MISC_BANKS = (0, 1, 2), (3, 4), 5, (6, 7)

        x_tok = sb("x_tok", [P, NT, E])
        ident = sb("ident", [P, P])
        ident_bf = sb("ident_bf", [P, P], BF16)
        wq_sb, wo_sb = sb("wq_sb", [P, E]), sb("wo_sb", [P, E])
        wdown_sb = sb("wdown_sb", [P, L])
        wk_sb, wv_sb = sb("wk_sb", [L, E]), sb("wv_sb", [L, E])
        nw_col = sb("nw_col", [P, 1])
        rw_row = sb("rw_row", [NE, E])
        rwT = sb("rwT", [P, NE])
        b1_row = sb("b1_row", [(NE + 1) * HT, P])
        b1T = sb("b1T", [P, (NE + 1) * HT])
        eb2_sb = sb("eb2_sb", [NE, E])
        sb2_sb = sb("sb2_sb", [1, E])
        ones_row = sb("ones_row", [1, P])
        before = sb("before", [P, NE, NE])
        minus_half = sb("minus_half", [P, QT])
        cos_sb, sin_sb = sb("cos_sb", [P, T]), sb("sin_sb", [P, T])
        swap_sb = sb("swap_sb", [P, P])
        W = H + HT * E
        Q_WORDS, K_WORDS = NP * T // 2, 2 * NP * T // 2
        S_WORDS = Q_WORDS + K_WORDS
        recycled = sb("recycled", [P, 2 * S_WORDS])
        w_sb = recycled[:, 0:(NE + 1) * W].rearrange("p (f w) -> p f w", w=W)
        FIRST_FFNS = S_WORDS // W
        xnT = sb("xnT", [P, NT, P])
        comb = sb("comb", [P, NT, NE])

        PE, ACTE, DVE, POOL, SP = (Lane(e, sem(n), n == "pool") for n, e in (
            ("pe", nc.tensor), ("act", nc.scalar), ("dve", nc.vector), ("pool", nc.gpsimd),
            ("sp", nc.sync)))
        c_const = Counter(sem("c_const"))
        c_x = [Counter(sem(f"c_x{b}")) for b in range(B)]
        c_mask = [Counter(sem(f"c_mask{i}")) for i in range(NSTACK)]
        c_store = [Counter(sem(f"c_store{i}")) for i in range(2)]
        c_stack = [Counter(sem(f"c_stack{i}")) for i in range(NSTACK)]
        c_mst = [Counter(sem(f"c_mst{i}")) for i in range(2)]
        c_mld = [Counter(sem(f"c_mld{i}")) for i in range(NSTACK)]
        c_w = Counter(sem("c_w"))
        c_maskin = Counter(sem("c_maskin"))
        c_out = [Counter(sem(f"c_out{i}")) for i in range(2)]

        scr_qk = nc.dram_tensor("scr_qk", [B, 2, P, PARTS, T], BF16, kind="Internal").ap()
        scr_m = nc.dram_tensor("scr_m", [B, PARTS * N_HEAD, T], BF16, kind="Internal").ap()

        x_v = x.rearrange("b (q p) e -> b p q e", p=P)
        for b in range(2):
            SP.dma(x_tok[:, b * QT:(b + 1) * QT, :], x_v[b], c_x[b])
        for dst, src in ((ident[:, :], ident_in), (wdown_sb[:, :], w_down), (wq_sb[:, :], wq),
                         (wk_sb[:, :], wk_up), (wv_sb[:, :], wv_up), (swap_sb[:, :], rope_swap),
                         (cos_sb[:, :], rope_cos), (sin_sb[:, :], rope_sin),
                         (wo_sb[:, :], wo),
                         (nw_col[:, :], norm_weight.rearrange("(p a) -> p a", a=1)),
                         (rw_row[:, :], router_w),
                         (b1_row[0:HT, :], sb1.rearrange("(t p) -> t p", p=P)),
                         (b1_row[HT:, :], eb1.rearrange("e (t p) -> (e t) p", p=P)),
                         (eb2_sb[:, :], eb2), (sb2_sb[:, :], sb2.rearrange("(a n) -> a n", a=1)),
                         (ones_row[:, :], ones_row_in),
                         (before[:, :, :], before_in)):
            SP.dma(dst, src, c_const)
        consts = c_const.all()
        for b in range(2, B):
            SP.dma(x_tok[:, b * QT:(b + 1) * QT, :], x_v[b], c_x[b])

        def load_weights(ffns, after):
            for f in ffns:
                w1, w2 = (sw1, sw2) if f == 0 else (ew1[f - 1], ew2[f - 1])
                SP.dma(w_sb[:, f, 0:H], w1, c_w, after)
                SP.dma(w_sb[:, f, H:W].rearrange("p (t o) -> p t o", o=E),
                       w2.rearrange("(t p) o -> p t o", p=P), c_w)

        att = ExitStack()

        def asb(name, shape, dt=F32):
            return att.enter_context(nc.sbuf_tensor(name, shape, dt))

        stack1 = asb("stack1", [P, S_WORDS])
        stack_mem = [recycled[:, S_WORDS:2 * S_WORDS], stack1[:, :], recycled[:, 0:S_WORDS]]
        q_stack = [m[:, 0:Q_WORDS].bitcast(BF16).rearrange("p (j t) -> p j t", t=T) for m in stack_mem]
        k_stack = [m[:, Q_WORDS:S_WORDS].bitcast(BF16).rearrange("p (h j t) -> p h j t", h=2, t=T)
                   for m in stack_mem]
        v_aug = [asb(f"v_aug{i}", [P, QT, N_HEAD, VW]) for i in range(2)]
        probs = asb("probs", [P, NPROB, T])
        mask_f32 = asb("mask_f32", [N_MASK, 2, T])
        mask_bf = asb("mask_bf", [N_MASK, 2, T], BF16)
        xT = [asb(f"xT{i}", [P, T]) for i in range(1)]
        latT = [asb(f"latT{i}", [L, T]) for i in range(NSTACK)]
        raw = asb("raw", [P, T])
        turned = asb("turned", [P, T])
        parts = [[asb(f"parts{i}{n}", [P, PARTS, T], BF16) for n in "qk"] for i in range(1)]
        rest = [asb(f"rest{i}", [P, T]) for i in range(2)]
        mx = [asb(f"mx{i}", [P, QT, N_HEAD]) for i in range(2)]
        m_rest = asb("m_rest", [P, QT, N_HEAD])
        m_parts = asb("m_parts", [P, QT, PARTS * N_HEAD], BF16)
        mT = asb("mT", [PARTS * N_HEAD, T], BF16)
        outT = [asb(f"outT{i}", [P, NG, T]) for i in range(1)]
        rsum = asb("rsum", [P, N_HEAD])
        attn = asb("attn", [P, QT, E])
        attnT = asb("attnT", [P, T])
        stats = asb("stats", [P, QT, 6])
        moments = asb("moments", [P, QT, 2])
        rstd = asb("rstd", [P, QT])
        squares = asb("squares", [P, E])
        ssum = asb("ssum", [P, QT])
        rms = asb("rms", [P, QT])
        xn = asb("xn", [P, QT, E])
        logit_exp = asb("logit_exp", [P, QT, NE])
        gate = asb("gate", [P, QT, NE])
        above = asb("above", [P, QT, NE, NE])
        equal = asb("equal", [P, QT, NE, NE])
        rank = asb("rank", [P, QT, NE])
        picked = asb("picked", [P, QT, NE])
        gsum = asb("gsum", [P, QT])

        t_mask = SP.dma(mask_f32[:, :, :], mask_rows.rearrange("s n t -> n s t"), c_maskin)
        t_cast = DVE.do(lambda e: e.tensor_copy(mask_bf[:, :, :], mask_f32[:, :, :]), [t_mask])
        t_identb = DVE.do(lambda e: e.tensor_copy(ident_bf[:, :], ident[:, :]), [consts])
        stack_ready = []

        def prepare_stack(i):
            lane = DVE if i == 0 else POOL
            tz = [lane.do(lambda e, i=i: e.memset(stack_mem[i].bitcast(U32), 0), [lane.latest()])]
            for hp in range(2):
                lane.do(lambda e, i=i, hp=hp: e.memset(
                    k_stack[i][HALF * hp:HALF * hp + PARTS, hp, :, :], 1.0), tz + [lane.latest()])
                r = HALF * hp + ROW_MASK
                for s, stack in ((0, q_stack[i][r:r + N_MASK, :, :]), (1, k_stack[i][r:r + N_MASK, hp, :, :])):
                    src = mask_bf[:, s:s + 1, :].broadcast_to([N_MASK, NP, T])
                    SP.dma(stack, src, c_mask[i], [t_cast] + tz)
            stack_ready.append([c_mask[i].all(), (lane.sem, lane.count)])

        prepare_stack(0)
        for v in range(2):
            t_v0 = DVE.do(lambda e: e.memset(v_aug[v][:, :, :, :].bitcast(U32), 0))
            t_v1 = DVE.do(lambda e: e.memset(v_aug[v][:, :, :, D:D + 1], 1.0), [t_v0])
        t_half = DVE.do(lambda e: e.memset(minus_half[:, :], -0.5))
        v_free = [t_v1, t_v1]

        misc_state = {"next": 0, "free": [None] * len(MISC_BANKS)}

        def misc_take():
            n = misc_state["next"]
            misc_state["next"] = (n + 1) % len(MISC_BANKS)
            return n, psum[:, MISC_BANKS[n], :], misc_state["free"][n]

        def misc_free(n, token):
            misc_state["free"][n] = token

        n, bank, free = misc_take()
        PE.do(lambda e: e.transpose(bank[:, 0:NE], rw_row[:, :], ident[0:NE, 0:NE]), [consts], False)
        t = PE.do(lambda e: e.transpose(bank[:, P:P + (NE + 1) * HT], b1_row[:, :],
                                        ident[0:(NE + 1) * HT, 0:(NE + 1) * HT]))
        DVE.do(lambda e: e.tensor_copy(rwT[:, :], bank[:, 0:NE]), [t])
        t_wT = DVE.do(lambda e: e.tensor_copy(b1T[:, :], bank[:, P:P + (NE + 1) * HT]))
        misc_free(n, t_wT)

        state = {k: {} for k in ("stored", "loaded", "m_loaded", "x_done", "m_done", "latT", "v",
                                 "outT", "mx_free", "pv", "normed")}
        last = {"xT": None, "raw": None, "attn": None, "attnT": None, "outT_free": None,
                "latT": [None] * NSTACK, "parts_free": [None, None], "mT_free": None,
                "m_parts_free": None, "mx_free": [None, None], "rest": [None, None]}

        def project(b):
            n, bank, free = misc_take()
            for j in range(QT):
                t = PE.do(lambda e, j=j: e.transpose(bank[:, j * P:(j + 1) * P], x_tok[:, b * QT + j, :],
                                                     ident[:, :]),
                          [free, c_x[b].all(), consts] if j == 0 else (), j == QT - 1)
            yield
            t_xT = ACTE.do(lambda e: e.activation(xT[0][:, :], bank, ACT.Copy), [t, last["xT"]])
            misc_free(n, t_xT)
            yield
            n, bank2, free = misc_take()
            t = PE.do(lambda e: e.matmul(bank2[0:L, :], wdown_sb[:, :], xT[0][:, :], start=True, stop=True),
                      [free, t_xT])
            yield
            t_lat = ACTE.do(lambda e: e.activation(latT[b % NSTACK][:, :], bank2[0:L, :], ACT.Copy),
                            [t, last["latT"][b % NSTACK]])
            misc_free(n, t_lat)
            state["latT"][b] = t_lat
            for s, (w_sb, src) in enumerate(((wq_sb[:, :], xT[0][:, :]), (wk_sb[:, :], latT[b % NSTACK][:, :]))):
                n, bank3, free = misc_take()
                t = PE.do(lambda e, w_sb=w_sb, src=src, bank3=bank3: e.matmul(bank3, w_sb, src, start=True, stop=True),
                          [free, t_lat, t_xT])
                if s == 0:
                    last["xT"] = t
                yield
                t_raw = ACTE.do(lambda e, bank3=bank3, s=s: e.activation(raw[:, :], bank3, ACT.Copy,
                                                                      scale=SCALE if s == 0 else 1.0),
                                [t, last["raw"]])
                misc_free(n, t_raw)
                yield
                n, bank4, free = misc_take()
                t = PE.do(lambda e, bank4=bank4: e.matmul(bank4, swap_sb[:, :], raw[:, :], start=True, stop=True),
                          [free, t_raw])
                t_c = POOL.do(lambda e: e.tensor_tensor(raw[:, :], raw[:, :], cos_sb[:, :], ALU.mult), [t])
                yield
                t_s = DVE.do(lambda e, bank4=bank4: e.tensor_tensor(turned[:, :], bank4, sin_sb[:, :], ALU.mult),
                             [t, last["rest"][0]])
                misc_free(n, t_s)
                yield
                t_r = DVE.do(lambda e: e.tensor_tensor(turned[:, :], turned[:, :], raw[:, :], ALU.add),
                             [t_c, t_s])
                last["raw"] = t_r
                pt = parts[0][s]
                t_h = ACTE.do(lambda e, pt=pt: e.activation(pt[:, 0, :], turned[:, :], ACT.Copy),
                              [t_r, last["parts_free"][s]])
                yield
                t_r1 = POOL.do(lambda e, pt=pt: e.tensor_tensor(rest[0][:, :], turned[:, :], pt[:, 0, :],
                                                                ALU.subtract), [t_h])
                last["rest"][0] = t_r1
                t_m = POOL.do(lambda e, pt=pt: e.tensor_copy(pt[:, 1, :], rest[0][:, :]), [t_r1])
                t_l = POOL.do(lambda e, pt=pt: e.tensor_tensor(pt[:, 2, :], rest[0][:, :], pt[:, 1, :],
                                                               ALU.subtract), [t_m])
                t_st = SP.dma(scr_qk[b, s], pt[:, :, :], c_store[s], [t_l])
                last["parts_free"][s] = t_st
                yield
            state["stored"][b] = [c_store[0].all(), c_store[1].all()]

        def load_stacks(b):
            i = b % NSTACK
            gate_ = [state["x_done"].get(b - NSTACK)]
            for hp in range(2):
                t_z = POOL.do(lambda e, hp=hp: e.memset(
                    q_stack[i][HALF * hp:HALF * hp + PARTS, :, :].bitcast(U32), 0),
                    gate_ + stack_ready[i] + [POOL.latest()])
            first = gate_ + stack_ready[i] + state["stored"][b]
            for s in range(2):
                for hp in range(2):
                    src = scr_qk[b, s].rearrange("(j h d) c t -> h c d j t", h=2, d=D)[hp]
                    for n, term in enumerate(TERMS):
                        r = HALF * hp + ROW_TERM + D * n
                        dst = (q_stack[i][r:r + D, :, :] if s == 0 else k_stack[i][r:r + D, hp, :, :])
                        SP.dma(dst, src[term[s]], c_stack[i], first)
            state["loaded"][b] = [c_stack[i].all(), t_z]

        def values(b):
            n, bank, free = misc_take()
            for j in range(QT):
                t = PE.do(lambda e, j=j: e.matmul(bank[:, j * P:(j + 1) * P], latT[b % NSTACK][:, j * P:(j + 1) * P],
                                                  wv_sb[:, :], start=True, stop=True),
                          [free, state["latT"][b]] if j == 0 else (), j == QT - 1)
            last["latT"][b % NSTACK] = t
            yield
            yield
            t_v = ACTE.do(lambda e: e.activation(
                v_aug[b % 2][:, :, :, 0:D], bank.rearrange("p (q h d) -> p q h d", q=QT, d=D), ACT.Copy),
                [t, v_free[b % 2]])
            misc_free(n, t_v)
            state["v"][b] = t_v

        def place_maxima(b):
            m = mx[b % 2]
            neg = m_parts
            part = lambda c: neg[:, :, c * N_HEAD:(c + 1) * N_HEAD]
            t1 = DVE.do(lambda e: e.tensor_scalar(part(0), m[:, :, :], -1.0, None, ALU.mult),
                        [state["m_done"][b], last["m_parts_free"]])
            t2 = DVE.do(lambda e: e.scalar_tensor_tensor(out=m_rest[:, :, :], in0=m[:, :, :], scalar=-1.0,
                                                         in1=part(0), op0=ALU.mult, op1=ALU.subtract), [t1])
            last["mx_free"][b % 2] = t2
            t3 = DVE.do(lambda e: e.tensor_copy(part(1), m_rest[:, :, :]), [t2])
            t4 = DVE.do(lambda e: e.tensor_tensor(part(2), m_rest[:, :, :], part(1), ALU.subtract), [t3])
            yield
            n, bank, free = misc_take()
            bank_bf = bank.bitcast(BF16)
            for j in range(QT):
                t = PE.do(lambda e, j=j: e.transpose(bank_bf[0:PARTS * N_HEAD, j * P:(j + 1) * P],
                                                     neg[:, j, :], ident_bf[:, :]),
                          [free, t4, t_identb] if j == 0 else (), j == QT - 1)
            last["m_parts_free"] = t
            yield
            t5 = ACTE.do(lambda e: e.activation(mT[:, :], bank_bf[0:PARTS * N_HEAD, 0:T], ACT.Copy),
                         [t, last["mT_free"]])
            misc_free(n, t5)
            t6 = SP.dma(scr_m[b], mT[:, :], c_mst[b % 2], [t5])
            last["mT_free"] = t6
            for hp in range(2):
                SP.dma(q_stack[b % NSTACK][HALF * hp:HALF * hp + PARTS, :, :],
                       scr_m[b].rearrange("(c j h) t -> h c j t", c=PARTS, h=2)[hp],
                       c_mld[b % NSTACK], [t6, state["m_done"][b]])
            state["m_loaded"][b] = c_mld[b % NSTACK].all()
            yield

        def finish(b):
            tiles = slice(b * QT, (b + 1) * QT)
            t_attn = []
            for j in range(QT):
                n, bank, free = misc_take()
                for g in range(NG):
                    t = PE.do(lambda e, g=g, j=j, bank=bank: e.transpose(
                        bank[:, g * P:(g + 1) * P], outT[0][:, g, j * P:(j + 1) * P], ident[:, :]),
                        [free, state["outT"][b]] if g == 0 else (), g == NG - 1)
                yield
                heads = bank.rearrange("p (h c) -> p h c", c=VW)
                t_rs = DVE.do(lambda e, heads=heads: e.reciprocal(rsum[:, :], heads[:, :, D]),
                              [t] + t_attn[-1:])
                t_a = DVE.do(lambda e, heads=heads, j=j: e.tensor_tensor(
                    attn[:, j, :].rearrange("p (h d) -> p h d", d=D), heads[:, :, 0:D],
                    rsum[:, :].unsqueeze(2).broadcast_to([P, N_HEAD, D]), ALU.mult), [t_rs, last["attn"]])
                t_attn.append(t_a)
                misc_free(n, t_a)
                yield
            last["outT_free"] = t
            n, bank, free = misc_take()
            for j in range(QT):
                t = PE.do(lambda e, j=j, bank=bank: e.transpose(bank[:, j * P:(j + 1) * P], attn[:, j, :], ident[:, :]),
                          [free, t_attn[-1]] if j == 0 else (), j == QT - 1)
            last["attn"] = t
            yield
            t_aT = ACTE.do(lambda e, bank=bank: e.activation(attnT[:, :], bank, ACT.Copy), [t, last["attnT"]])
            misc_free(n, t_aT)
            yield
            n, bank, free = misc_take()
            for j in range(QT):
                t = PE.do(lambda e, j=j, bank=bank: e.matmul(bank[:, j * P:(j + 1) * P], attnT[:, j * P:(j + 1) * P],
                                                  wo_sb[:, :], start=True, stop=True),
                          [free, t_aT] if j == 0 else (), j == QT - 1)
            last["attnT"] = t
            yield
            rows = x_tok[:, tiles, :]
            t_y = DVE.do(lambda e, bank=bank: e.tensor_tensor(rows, bank.rearrange("p (q e) -> p q e", q=QT), rows,
                                                   ALU.add), [t])
            misc_free(n, t_y)
            yield
            for j in range(QT - 1):
                DVE.do(lambda e, j=j: e.bn_stats(stats[:, j, :], x_tok[:, b * QT + j, :]), [t_y], False)
            t_s = DVE.do(lambda e: e.bn_stats(stats[:, QT - 1, :], x_tok[:, b * QT + QT - 1, :]))
            for j in range(QT):
                t_m = DVE.do(lambda e, j=j: e.bn_aggr(moments[:, j, :], stats[:, j, :]), [t_s])
            yield
            t1 = POOL.do(lambda e: e.tensor_scalar(rstd[:, :], moments[:, :, 1], LN_EPS, None, ALU.add), [t_m])
            t2 = POOL.do(lambda e: e.tensor_tensor(rstd[:, :], rstd[:, :], minus_half[:, :], ALU.pow),
                         [t1, t_half])
            yield
            for j in range(QT):
                t_n = DVE.do(lambda e, j=j: e.tensor_scalar(
                    x_tok[:, b * QT + j, :], x_tok[:, b * QT + j, :], moments[:, j, 0:1], rstd[:, j:j + 1],
                    ALU.subtract, ALU.mult), [t2], j == QT - 1)
            yield
            for j in range(QT):
                t_q = DVE.do(lambda e, j=j: e.tensor_tensor_reduce(
                    squares[:, :], x_tok[:, b * QT + j, :], x_tok[:, b * QT + j, :], 1.0, 0.0,
                    ALU.mult, ALU.add, ssum[:, j:j + 1]), [t_n] if j == 0 else [t_q])
            yield
            t1 = POOL.do(lambda e: e.tensor_scalar(rms[:, :], ssum[:, :], 1.0 / E, RMS_EPS, ALU.mult, ALU.add), [t_q])
            t2 = POOL.do(lambda e: e.tensor_tensor(rms[:, :], rms[:, :], minus_half[:, :], ALU.pow), [t1])
            yield
            for j in range(QT):
                t_xn = DVE.do(lambda e, j=j: e.tensor_scalar(
                    xn[:, j, :], x_tok[:, b * QT + j, :], rms[:, j:j + 1], None, ALU.mult),
                    [t2, state["normed"].get(b - 1)], j == QT - 1)
            yield
            n, bank, free = misc_take()
            for j in range(QT):
                t = PE.do(lambda e, j=j, bank=bank: e.transpose(bank[:, j * P:(j + 1) * P], xn[:, j, :], ident[:, :]),
                          [free, t_xn] if j == 0 else (), j == QT - 1)
            state["normed"][b] = t
            yield
            t_xnT = ACTE.do(lambda e, bank=bank: e.activation(
                xnT[:, tiles, :].rearrange("p q t -> p (q t)"), bank, ACT.Copy, scale=nw_col[:, 0:1]),
                [t, consts])
            misc_free(n, t_xnT)
            yield
            n, bank, free = misc_take()
            for j in range(QT):
                t = PE.do(lambda e, j=j, bank=bank: e.matmul(bank[:, j * NE:(j + 1) * NE], xnT[:, b * QT + j, :],
                                                  rwT[:, :], start=True, stop=True),
                          [free, t_xnT, t_wT] if j == 0 else (), j == QT - 1)
            yield
            t_e = ACTE.do(lambda e, bank=bank: e.activation(logit_exp[:, :, :].rearrange("p q n -> p (q n)"),
                                                 bank[:, 0:QT * NE], ACT.Exp, scale=-1.0), [t])
            misc_free(n, t_e)
            yield
            t1 = DVE.do(lambda e: e.tensor_scalar(logit_exp[:, :, :], logit_exp[:, :, :], 1.0, None, ALU.add), [t_e])
            t2 = DVE.do(lambda e: e.reciprocal(gate[:, :, :], logit_exp[:, :, :]), [t1])
            mine = gate[:, :, :].unsqueeze(3).broadcast_to([P, QT, NE, NE])
            other = gate[:, :, :].unsqueeze(2).broadcast_to([P, QT, NE, NE])
            earlier = before[:, :, :].unsqueeze(1).broadcast_to([P, QT, NE, NE])
            t3 = DVE.do(lambda e: e.tensor_tensor(above[:, :, :, :], other, mine, ALU.is_gt), [t2])
            t4 = DVE.do(lambda e: e.tensor_tensor(equal[:, :, :, :], other, mine, ALU.is_equal))
            yield
            t5 = DVE.do(lambda e: e.tensor_tensor(equal[:, :, :, :], equal[:, :, :, :], earlier, ALU.mult), [t4, consts])
            t6 = DVE.do(lambda e: e.tensor_tensor(above[:, :, :, :], above[:, :, :, :], equal[:, :, :, :], ALU.add), [t5])
            t7 = DVE.do(lambda e: e.tensor_reduce(rank[:, :, :], above[:, :, :, :], AXIS_X, ALU.add), [t6])
            yield
            t8 = DVE.do(lambda e: e.scalar_tensor_tensor(out=picked[:, :, :], in0=rank[:, :, :], scalar=float(TOPK),
                                                         in1=gate[:, :, :], op0=ALU.is_lt, op1=ALU.mult), [t7])
            t9 = DVE.do(lambda e: e.tensor_reduce(gsum[:, :], picked[:, :, :], AXIS_X, ALU.add), [t8])
            t10 = DVE.do(lambda e: e.tensor_scalar(gsum[:, :], gsum[:, :], TOPK_EPS, None, ALU.add), [t9])
            t11 = DVE.do(lambda e: e.reciprocal(gsum[:, :], gsum[:, :]), [t10])
            t12 = DVE.do(lambda e: e.tensor_tensor(comb[:, tiles, :], picked[:, :, :],
                                                   gsum[:, :].unsqueeze(2).broadcast_to([P, QT, NE]), ALU.mult), [t11])
            yield

        ring = {"exp": 0, "max": 0}
        exp_free = [None] * len(EXP_BANKS)
        max_free = [None] * len(MAX_BANKS)
        probs_free = [None] * NPROB
        pv_free = [None]
        exp_tok = {}

        def exp_slot(G, s):
            b, g = divmod(G, NG)
            qs, ks = q_stack[b % NSTACK], k_stack[b % NSTACK]
            r = ring["exp"] % len(EXP_BANKS)
            ring["exp"] += 1
            bank = psum[:, EXP_BANKS[r], :]
            if s < GH:
                plan = [(g * GH + s, 0, 0)]
            elif s < 2 * GH:
                plan = [(g * GH + s - GH, 1, 0), (g * GH + s - GH, 3, 3 * P)]
            else:
                plan = [(g * GH + 2 * (s - 2 * GH) + i, 2, 2 * P * i) for i in range(2)]
            for n, (h, kt, at) in enumerate(plan):
                j, hp = divmod(h, 2)
                width = T - kt * P
                t = PE.do(lambda e, j=j, hp=hp, kt=kt, at=at, width=width: e.matmul(
                    bank[:, at:at + width], ks[:, hp, j, kt * P:(kt + 1) * P], qs[:, j, kt * P:T],
                    start=True, stop=True),
                    [exp_free[r], state["m_loaded"][b]] if n == 0 else (), n == len(plan) - 1)
            if s == SLOTS - 1 and g == NG - 1:
                state["x_done"][b] = t
            held = (G * SLOTS + s) % NPROB
            te = ACTE.do(lambda e: e.activation(probs[:, held, :], bank, ACT.Exp),
                         [t, probs_free[held]])
            exp_free[r] = te
            exp_tok[G, s] = te

        def pv(G, kt):
            b, g = divmod(G, NG)
            at = {0: (0, 0), 1: (GH, 0), 3: (GH, 3 * P)}
            need = [exp_tok[G, {0: GH - 1, 1: 2 * GH - 1, 3: 2 * GH - 1, 2: SLOTS - 1}[kt]]]
            if kt == 0:
                need += [pv_free[0], state["v"][b]]
            for i in range(GH):
                h = g * GH + i
                width = T - kt * P
                s, c = (2 * GH + i // 2, 2 * P * (i % 2)) if kt == 2 else (at[kt][0] + i, at[kt][1])
                t = PE.do(lambda e, i=i, h=h, s=s, c=c, width=width: e.matmul(
                    psum[VW * i:VW * (i + 1), PV_BANK, kt * P:T], v_aug[b % 2][:, kt, h, :],
                    probs[:, (G * SLOTS + s) % NPROB, c:c + width], start=(kt == 0), stop=(kt == 2),
                    skip_group_check=True, tile_position=(0, VW * i)), need if i == 0 else (), i == GH - 1)
            done = {0: range(GH), 1: (), 3: range(GH, 2 * GH), 2: range(2 * GH, SLOTS)}[kt]
            for s in done:
                probs_free[(G * SLOTS + s) % NPROB] = t
            if kt == 2:
                state["pv"][G] = t
                if g == NG - 1:
                    v_free[b % 2] = t

        def pv_out(G):
            b, g = divmod(G, NG)
            t = ACTE.do(lambda e: e.activation(outT[0][:, g, :], psum[:, PV_BANK, :], ACT.Copy),
                        [state["pv"][G], last["outT_free"]])
            pv_free[0] = t
            state["outT"][b] = t

        def max_slot(G, s):
            b, g = divmod(G, NG)
            qs, ks = q_stack[b % NSTACK], k_stack[b % NSTACK]
            r = ring["max"] % len(MAX_BANKS)
            ring["max"] += 1
            bank = psum[:, MAX_BANKS[r], :]
            if s < GH:
                plan = [(g * GH + s, 3, 0)]
            elif s < 2 * GH:
                plan = [(g * GH + s - GH, 2, 0), (g * GH + s - GH, 0, 3 * P)]
            else:
                plan = [(g * GH + 2 * (s - 2 * GH) + i, 1, 2 * P * i) for i in range(2)]
            for n, (h, qt, at) in enumerate(plan):
                j, hp = divmod(h, 2)
                width = (qt + 1) * P
                t = PE.do(lambda e, j=j, hp=hp, qt=qt, at=at, width=width: e.matmul(
                    bank[:, at:at + width], qs[:, j, qt * P:(qt + 1) * P], ks[:, hp, j, 0:width],
                    start=True, stop=True),
                    [max_free[r]] + state["loaded"][b] if n == 0 else (), n == len(plan) - 1)
            m = mx[b % 2]
            need = [t, last["mx_free"][b % 2]]
            if s < 2 * GH:
                for h, qt, at in plan:
                    width = (qt + 1) * P
                    t = DVE.do(lambda e, h=h, qt=qt, at=at, width=width: e.tensor_reduce(
                        m[:, qt, h:h + 1], bank[:, at:at + width], AXIS_X, ALU.max), need)
            else:
                h = plan[0][0]
                t = DVE.do(lambda e: e.tensor_reduce(
                    m[:, 1, h:h + 2], bank.rearrange("p (h k) -> p h k", h=2), AXIS_X, ALU.max), need)
            max_free[r] = t
            if s == SLOTS - 1 and g == NG - 1:
                state["m_done"][b] = t

        background = deque()

        def advance():
            while background:
                if next(background[0], "done") == "done":
                    background.popleft()
                    continue
                return

        def run_all():
            while background:
                advance()

        background.append(project(0))
        run_all()
        load_stacks(0)
        for i in range(1, NSTACK):
            prepare_stack(i)
        for idx in range(-LEAD, B * NG + 1):
            X, M = idx, idx + LEAD
            b, g = divmod(idx, NG)
            if g == 2 and 0 <= b + 1 < B:
                background.appendleft(place_maxima(b + 1))
                advance()
            if g == 3 and 0 <= b + 1 < B:
                background.append(values(b + 1))
            if g == 0 and 0 < b + 2 < B:
                run_all()
                load_stacks(b + 2)
            if g == 0 and b - 1 == B - NSTACK:
                load_weights(range(FIRST_FFNS), [state["x_done"][b - 1]])
            if g == 0 and b - 1 == B - NSTACK + 1:
                load_weights(range(FIRST_FFNS, NE + 1), [state["x_done"][b - 1]])
            if idx == -LEAD:
                background.append(project(1))
            if g == 1 and 2 < b + 3 < B or idx == -3:
                background.append(project(max(b + 3, 2)))
            for s in range(SLOTS):
                if 0 <= X < B * NG:
                    if s == 0 and g == 0:
                        run_all()
                    exp_slot(X, s)
                if 0 <= M < B * NG:
                    max_slot(M, s)
                if s == 6 and 0 <= X < B * NG:
                    pv(X, 0)
                if s == 9 and 0 <= X < B * NG:
                    pv(X, 1)
                if s == 0 and 1 <= X <= B * NG:
                    pv(X - 1, 3)
                if s == 1 and 1 <= X <= B * NG:
                    pv(X - 1, 2)
                if s == 3 and 1 <= X <= B * NG:
                    pv_out(X - 1)
                    if g == 0:
                        background.append(finish(b - 1))
                advance()
        run_all()

        weights = c_w.all()
        att_end = [(ln.sem, ln.count) for ln in (PE, ACTE, DVE, POOL)]
        att.close()

        def fsb(name, shape, dt=F32):
            return ctx.enter_context(nc.sbuf_tensor(name, shape, dt))

        hT = [fsb(f"hT{i}", [P, HT, T]) for i in range(2)]
        acc = [fsb(f"acc{i}", [P, QT, E]) for i in range(2)]
        combT = [fsb(f"combT{i}", [NE, QT, P]) for i in range(2)]
        f_stats = fsb("f_stats", [P, QT, 6])
        f_moments = fsb("f_moments", [P, QT, 2])
        f_rstd = fsb("f_rstd", [P, QT])
        H_BANKS, Y_BANKS = (0, 1, 2, 3, 4), (5, 6, 7)
        h_free, y_free = [None] * len(H_BANKS), [None] * len(Y_BANKS)
        ht_free = [None, None]
        acc_free = [None, None]
        for ln in (PE, ACTE, DVE, POOL):
            ln.wait(att_end)
        units = [(b, f) for b in range(B) for f in range(NE + 1)]
        h_tok = {}
        hn = 0
        acc_tok = None
        for u in range(len(units) + 1):
            if u < len(units):
                b, f = units[u]
                tiles = slice(b * QT, (b + 1) * QT)
                for t4 in range(HT):
                    r = hn % len(H_BANKS)
                    hn += 1
                    t = PE.do(lambda e, f=f, t4=t4, r=r, tiles=tiles: e.matmul(
                        psum[:, H_BANKS[r], :], w_sb[:, f, t4 * P:(t4 + 1) * P],
                        xnT[:, tiles, :].rearrange("p q t -> p (q t)"), start=True, stop=True),
                        [h_free[r], weights])
                    bias = b1T[:, f * HT + t4:f * HT + t4 + 1]
                    dst = hT[u % 2][:, t4, :]
                    if t4 % 4 != 3:
                        t = ACTE.do(lambda e, dst=dst, r=r, bias=bias: e.activation(
                            dst, psum[:, H_BANKS[r], :], ACT.Relu, bias=bias), [t, ht_free[u % 2]])
                    else:
                        t = DVE.do(lambda e, dst=dst, r=r, bias=bias: e.tensor_scalar(
                            dst, psum[:, H_BANKS[r], :], bias, 0.0, ALU.add, ALU.max), [t, ht_free[u % 2]])
                    h_free[r] = t
                    h_tok.setdefault(u, []).append(t)
            if u < len(units) and f == 0:
                r = hn % len(H_BANKS)
                hn += 1
                for j in range(QT):
                    t = PE.do(lambda e, j=j, r=r, b=b: e.transpose(
                        psum[0:NE, H_BANKS[r], j * P:(j + 1) * P], comb[:, b * QT + j, :], ident[:, :]),
                        [h_free[r]], j == QT - 1)
                h_free[r] = t_cT = DVE.do(lambda e, r=r, b=b: e.tensor_copy(
                    combT[b % 2][:, :, :].rearrange("n q t -> n (q t)"), psum[0:NE, H_BANKS[r], :]), [t])
            if u > 0:
                v = u - 1
                b, f = units[v]
                r = v % len(Y_BANKS)
                need = h_tok.pop(v) + [y_free[r], t_cT]
                for j in range(QT):
                    dst = psum[:, Y_BANKS[r], j * P:(j + 1) * P]
                    for t4 in range(HT):
                        t = PE.do(lambda e, f=f, v=v, t4=t4, j=j, dst=dst: e.matmul(
                            dst, hT[v % 2][:, t4, j * P:(j + 1) * P], w_sb[:, f, H + t4 * E:H + (t4 + 1) * E],
                            start=(t4 == 0), stop=(t4 == HT - 1 and f > 0)), need,
                            f > 0 and j == QT - 1 and t4 == HT - 1)
                        need = ()
                    if f == 0:
                        PE.do(lambda e, dst=dst: e.matmul(dst, ones_row[:, :], sb2_sb[:, :],
                                                          start=False, stop=False), (), False)
                        t = PE.do(lambda e, dst=dst, b=b, j=j: e.matmul(
                            dst, combT[b % 2][:, j, :], eb2_sb[:, :], start=False, stop=True), (), j == QT - 1)
                ht_free[v % 2] = t
                a = acc[b % 2]
                bank = psum[:, Y_BANKS[r], :].rearrange("p (q e) -> p q e", q=QT)
                if f == 0:
                    rows = x_tok[:, b * QT:(b + 1) * QT, :]
                    acc_tok = DVE.do(lambda e, a=a, bank=bank, rows=rows: e.tensor_tensor(
                        a[:, :, :], bank, rows, ALU.add), [t, acc_free[b % 2]])
                else:
                    for j in range(QT):
                        tt = DVE.do(lambda e, a=a, bank=bank, j=j, f=f, b=b: e.scalar_tensor_tensor(
                            out=a[:, j, :], in0=bank[:, j, :], scalar=comb[:, b * QT + j, f - 1:f],
                            in1=a[:, j, :], op0=ALU.mult, op1=ALU.add), [t, acc_tok], j == QT - 1)
                    acc_tok = tt
                y_free[r] = acc_tok
                if f == NE:
                    for j in range(QT):
                        t_s = DVE.do(lambda e, j=j, a=a: e.bn_stats(f_stats[:, j, :], a[:, j, :]), [acc_tok], j == QT - 1)
                    for j in range(QT):
                        t_m = DVE.do(lambda e, j=j: e.bn_aggr(f_moments[:, j, :], f_stats[:, j, :]), [t_s], j == QT - 1)
                    t1 = POOL.do(lambda e: e.tensor_scalar(f_rstd[:, :], f_moments[:, :, 1], LN_EPS, None, ALU.add), [t_m])
                    t2 = POOL.do(lambda e: e.tensor_tensor(f_rstd[:, :], f_rstd[:, :], minus_half[:, :], ALU.pow), [t1])
                    for j in range(QT):
                        t_n = DVE.do(lambda e, j=j, a=a: e.tensor_scalar(
                            a[:, j, :], a[:, j, :], f_moments[:, j, 0:1], f_rstd[:, j:j + 1],
                            ALU.subtract, ALU.mult), [t2], j == QT - 1)
                    acc_free[b % 2] = SP.dma(out.rearrange("b (q p) e -> b p q e", p=P)[b], a[:, :, :], c_out[b % 2], [t_n])
        SP.wait([c.all() for c in c_out])



_INS = ["L0_attn_x", "L0_attn_wq", "L0_attn_w_down", "L0_attn_wk_up", "L0_attn_wv_up", "L0_attn_wo",
        "L0_ffn_norm_weight", "L0_ffn_router_w", "L0_ffn_sw1", "L0_ffn_sb1", "L0_ffn_sw2", "L0_ffn_sb2",
        "L0_ffn_ew1", "L0_ffn_eb1", "L0_ffn_ew2", "L0_ffn_eb2"]


def shape_constants(T, E, n_expert):
    D = E // N_HEAD
    inv = 1.0 / ROPE_THETA ** (np.arange(0, D, 2, dtype=np.float32) / D)
    ang = np.outer(np.arange(T, dtype=np.float32), inv)
    cos, sin = np.cos(ang).astype(np.float32), np.sin(ang).astype(np.float32)
    pair = (np.arange(E) % D) // 2
    sign = np.where(np.arange(E) % 2 == 0, -1.0, 1.0).astype(np.float32)
    rope_cos = np.ascontiguousarray(cos[:, pair].T)
    rope_sin = np.ascontiguousarray((sin[:, pair] * sign).T)
    swap = np.zeros((E, E), np.float32)
    swap[np.arange(E) ^ 1, np.arange(E)] = 1.0
    t = np.arange(T)
    mask_q, mask_k = [], []
    for tile in range(T // P):
        for page in range(1, P // PAGE):
            start = tile * P
            mask_q.append(np.where((t >= start) & (t < start + page * PAGE), MASK_BIG, 0.0))
            mask_k.append(((t >= start + page * PAGE) & (t < start + (page + 1) * PAGE)) * 1.0)
    mask = np.stack([np.stack(mask_q), np.stack(mask_k)]).astype(np.float32)
    e = np.arange(n_expert)
    before = np.broadcast_to((e[None, :] < e[:, None]).astype(np.float32), (P, n_expert, n_expert))
    return [rope_cos, rope_sin, swap, mask, np.eye(P, dtype=np.float32), np.ones((1, P), np.float32),
            np.ascontiguousarray(before)]


def kernel(**inputs):
    import numpy as _np
    import concourse.bacc as _bacc
    from concourse import mybir as _mybir
    from concourse.bass_utils import run_bass_kernel_spmd as _run

    nc = _bacc.Bacc("TRN2", target_bir_lowering=False, num_devices=1)
    arrays, args = {}, []

    def give(name, a):
        a = _np.ascontiguousarray(a)
        arrays[name] = a
        args.append(nc.dram_tensor(name, a.shape, _mybir.dt.from_np(a.dtype), kind="ExternalInput").ap())

    for name in _INS:
        give(f"in_{name}", inputs[name])
    B, T, E = inputs["L0_attn_x"].shape
    for i, a in enumerate(shape_constants(T, E, inputs["L0_ffn_ew1"].shape[0])):
        give(f"const_{i}", a)
    args.append(nc.dram_tensor("out", (B, T, E), F32, kind="ExternalOutput").ap())
    build(nc, *args)
    r = _run(nc, [arrays], core_ids=[0])
    return r.results[0]["out"]
```

```python
from contextlib import ExitStack

import numpy as np
import concourse.bass as bass
from concourse import mybir

F32 = mybir.dt.float32
BF16 = mybir.dt.bfloat16
F32R = mybir.dt.float32r
U32 = mybir.dt.uint32
ACT = mybir.ActivationFunctionType
ALU = mybir.AluOpType
AXIS_X = mybir.AxisListType.X

P = 128
N_HEAD = 16
PAGE = 32
ROPE_THETA = 10000.0
TOPK = 2
LN_EPS = 1e-5
RMS_EPS = 1e-8
TOPK_EPS = 1e-6

HALF = 64
PARTS = 3
TERMS = [(0, 0), (0, 1), (1, 0), (1, 1), (0, 2), (2, 0)]
MASK_BIG = -1.0e38


class Lane:

    def __init__(self, engine, sem, serial=False):
        self.serial = serial
        self.engine, self.sem, self.count, self.seen = engine, sem, 0, {}

    def wait(self, tokens):
        for t in tokens:
            if t is None:
                continue
            sem, value = t
            if self.seen.get(sem.name, 0) < value:
                self.seen[sem.name] = value
                self.engine.wait_ge(sem, value)

    def do(self, make, after=(), signal=True):
        self.wait(after)
        if self.serial:
            self.wait([self.latest()])
        ins = make(self.engine)
        if not signal:
            return None
        self.count += 1
        ins.then_inc(self.sem, 1)
        return (self.sem, self.count)

    def latest(self):
        return (self.sem, self.count)

    def dma(self, out, src, counter, after=()):
        self.wait(after)
        counter.count += 16
        self.engine.dma_start(out, src).then_inc(counter.sem, 16)
        return (counter.sem, counter.count)


class Counter:

    def __init__(self, sem):
        self.sem, self.count = sem, 0

    def all(self):
        return (self.sem, self.count)


def build(nc, x, wq, w_down, wk_up, wv_up, wo, norm_weight, router_w, sw1, sb1, sw2, sb2,
          ew1, eb1, ew2, eb2, rope_cos, rope_sin, rope_swap, mask_rows, ident_in,
          before_in, prior_in, region_in, thresholds_in, upto_in, tile_index_in, out):
    B, T, E = x.shape
    L = w_down.shape[1]
    D = E // N_HEAD
    NE, _, H = ew1.shape
    assert E == P and D == 8 and T == 512
    QT = T // P
    NT = B * QT
    HT = H // P
    NP = N_HEAD // 2
    GH = 4
    NG = N_HEAD // GH
    PPB = P // PAGE
    N_MASK = QT * (PPB - 1)
    ROW_TERM = PARTS
    ROW_MASK = ROW_TERM + D * len(TERMS)
    assert ROW_MASK + N_MASK <= HALF
    SCALE = 1.0 / float(np.sqrt(D))
    VW = 32
    SLOTS = 10
    LEAD = 6
    NSTACK = 3
    FT = 2 * P
    ROWS = NT * P + FT
    N_TILES = NT * P * TOPK // FT + NE - 1
    MAX_E_TILES = NT * P // FT
    NPROB = 12

    ctx = ExitStack()
    with ctx:
        def sb(name, shape, dt=F32):
            return ctx.enter_context(nc.sbuf_tensor(name, shape, dt))

        def sem(name):
            return ctx.enter_context(nc.semaphore(name))

        psum = ctx.enter_context(nc.psum_tensor("psum", [P, 8, 512], F32))
        EXP_BANKS, MAX_BANKS, PV_BANK, MISC_BANKS = (0, 1, 2), (3, 4), 5, (6, 7)

        x_tok = sb("x_tok", [P, NT, E])
        ident = sb("ident", [P, P])
        ident_bf = sb("ident_bf", [P, P], BF16)
        wq_sb, wo_sb = sb("wq_sb", [P, E]), sb("wo_sb", [P, E])
        wdown_sb = sb("wdown_sb", [P, L])
        wk_sb, wv_sb = sb("wk_sb", [L, E]), sb("wv_sb", [L, E])
        nw_rows = sb("nw_rows", [P, E])
        rw_row = sb("rw_row", [NE, E])
        rwT = sb("rwT", [P, NE])
        b1_row = sb("b1_row", [(NE + 1) * HT, P])
        b1T = sb("b1T", [P, (NE + 1) * HT])
        b2_row = sb("b2_row", [NE + 1, P])
        b2T = sb("b2T", [P, NE + 1])
        prior = sb("prior", [P, P])
        ones = sb("ones", [P, P])
        zeros = sb("zeros", [P, FT // P, E])
        region = sb("region", [P, NE])
        filled = sb("filled", [P, NE])
        thresholds = sb("thresholds", [P, NE, MAX_E_TILES])
        upto = sb("upto", [P, NE, NE])
        tile_index = sb("tile_index", [P, N_TILES, NE])
        row_of = sb("row_of", [P, TOPK, NT], U32)
        share = sb("share", [P, TOPK, NT])
        before = sb("before", [P, NE, NE])
        minus_half = sb("minus_half", [P, QT])
        W = H + HT * E
        Q_WORDS, K_WORDS = NP * T // 2, 2 * NP * T // 2
        S_WORDS = Q_WORDS + K_WORDS
        rec = ExitStack()
        recycled = rec.enter_context(nc.sbuf_tensor("recycled", [P, 2 * S_WORDS], F32, side="right"))
        w_sb = recycled[:, 0:(NE + 1) * W].rearrange("p (f w) -> p f w", w=W)
        FIRST_FFNS = S_WORDS // W
        xnT_hi = sb("xnT_hi", [P, NT, P], F32R)
        xnT_lo = sb("xnT_lo", [P, NT, P], F32R)

        outT = [sb("outT0", [P, NG, T])]
        rsum = sb("rsum", [P, N_HEAD])
        attn = sb("attn", [P, QT, E])
        attnT = sb("attnT", [P, T])
        stats = sb("stats", [P, QT, 6])
        moments = sb("moments", [P, QT, 2])
        rstd = sb("rstd", [P, QT])
        rms = sb("rms", [P, QT])
        xn = [sb(f"xn{i}", [P, QT, E]) for i in range(2)]
        xnT = sb("xnT", [P, T])
        gate = sb("gate", [P, QT, NE])
        above = sb("above", [P, QT, NE, NE])
        equal = sb("equal", [P, QT, NE, NE])
        rank = sb("rank", [P, QT, NE])
        chosen = sb("chosen", [P, QT, NE])
        row_all = sb("row_all", [P, QT, NE])
        picked = sb("picked", [P, 2 * TOPK, QT, NE])
        row_f = sb("row_f", [P, TOPK, QT])
        gsum = sb("gsum", [P, QT])

        att = ExitStack()

        def asb(name, shape, dt=F32):
            return att.enter_context(nc.sbuf_tensor(name, shape, dt))

        cos_sb, sin_sb = asb("cos_sb", [P, T]), asb("sin_sb", [P, T])
        swap_sb = asb("swap_sb", [P, P])

        PE, ACTE, DVE, POOL, SP = (Lane(e, sem(n), n == "pool") for n, e in (
            ("pe", nc.tensor), ("act", nc.scalar), ("dve", nc.vector), ("pool", nc.gpsimd),
            ("sp", nc.sync)))
        c_const = Counter(sem("c_const"))
        c_x = [Counter(sem(f"c_x{b}")) for b in range(B)]
        c_mask = [Counter(sem(f"c_mask{i}")) for i in range(NSTACK)]
        c_store = [Counter(sem(f"c_store{i}")) for i in range(2)]
        c_stack = [Counter(sem(f"c_stack{i}")) for i in range(NSTACK)]
        c_mst = [Counter(sem(f"c_mst{i}")) for i in range(2)]
        c_mld = [Counter(sem(f"c_mld{i}")) for i in range(NSTACK)]
        c_w = Counter(sem("c_w"))
        c_scatter = [Counter(sem(f"c_scatter{i}")) for i in range(2)]
        c_zero = Counter(sem("c_zero"))
        c_xs = [Counter(sem(f"c_xs{i}")) for i in range(3)]
        c_ys = [Counter(sem(f"c_ys{i}")) for i in range(3)]
        NGATHER = 8
        c_gather = [Counter(sem(f"c_gather{i}")) for i in range(NGATHER)]
        c_maskin = Counter(sem("c_maskin"))
        c_out = [Counter(sem(f"c_out{i}")) for i in range(2)]

        scr_qk = nc.dram_tensor("scr_qk", [B, 2, P, PARTS, T], BF16, kind="Internal").ap()
        xs_dram = nc.dram_tensor("xs_dram", [NE * ROWS + FT, E], F32, kind="Internal").ap()
        ys_dram = nc.dram_tensor("ys_dram", [N_TILES * FT, E], F32, kind="Internal").ap()
        scr_m = nc.dram_tensor("scr_m", [B, PARTS * N_HEAD, T], BF16, kind="Internal").ap()

        x_v = x.rearrange("b (q p) e -> b p q e", p=P)
        for b in range(2):
            SP.dma(x_tok[:, b * QT:(b + 1) * QT, :], x_v[b], c_x[b])
        for dst, src in ((ident[:, :], ident_in), (wdown_sb[:, :], w_down), (wq_sb[:, :], wq),
                         (wk_sb[:, :], wk_up), (wv_sb[:, :], wv_up), (swap_sb[:, :], rope_swap),
                         (cos_sb[:, :], rope_cos), (sin_sb[:, :], rope_sin),
                         (wo_sb[:, :], wo),
                         (nw_rows[:, :], norm_weight.rearrange("(a n) -> a n", a=1).broadcast_to([P, E])),
                         (rw_row[:, :], router_w),
                         (b1_row[0:HT, :], sb1.rearrange("(t p) -> t p", p=P)),
                         (b1_row[HT:, :], eb1.rearrange("e (t p) -> (e t) p", p=P)),
                         (b2_row[0:1, :], sb2.rearrange("(a n) -> a n", a=1)), (b2_row[1:, :], eb2),
                         (before[:, :, :], before_in), (prior[:, :], prior_in),
                         (region[:, :], region_in), (thresholds[:, :, :], thresholds_in),
                         (upto[:, :, :], upto_in), (tile_index[:, :, :], tile_index_in)):
            SP.dma(dst, src, c_const)
        consts = c_const.all()
        for b in range(2, B):
            SP.dma(x_tok[:, b * QT:(b + 1) * QT, :], x_v[b], c_x[b])

        def load_weights(ffns, after):
            for f in ffns:
                w1, w2 = (sw1, sw2) if f == 0 else (ew1[f - 1], ew2[f - 1])
                SP.dma(w_sb[:, f, 0:H], w1, c_w, after)
                SP.dma(w_sb[:, f, H:W].rearrange("p (t o) -> p t o", o=E),
                       w2.rearrange("(t p) o -> p t o", p=P), c_w)

        stack1 = asb("stack1", [P, S_WORDS])
        stack_mem = [recycled[:, S_WORDS:2 * S_WORDS], stack1[:, :], recycled[:, 0:S_WORDS]]
        q_stack = [m[:, 0:Q_WORDS].bitcast(BF16).rearrange("p (j t) -> p j t", t=T) for m in stack_mem]
        k_stack = [m[:, Q_WORDS:S_WORDS].bitcast(BF16).rearrange("p (h j t) -> p h j t", h=2, t=T)
                   for m in stack_mem]
        v_aug = [asb(f"v_aug{i}", [P, QT, N_HEAD, D + 1]) for i in range(2)]
        probs = asb("probs", [P, NPROB, T])
        mask_f32 = probs[0:N_MASK, 0:2, :]
        mask_bf = probs[0:N_MASK, 2:3, :].bitcast(BF16).rearrange("n a (s t) -> n (a s) t", s=2)
        xT = [asb(f"xT{i}", [P, T]) for i in range(1)]
        latT = [asb(f"latT{i}", [L, T]) for i in range(NSTACK)]
        raw = asb("raw", [P, T])
        turned = asb("turned", [P, T])
        parts = asb("parts", [P, PARTS, T], BF16)
        mx = [asb(f"mx{i}", [P, QT, N_HEAD]) for i in range(2)]
        m_rest = asb("m_rest", [P, QT, N_HEAD])
        m_parts = asb("m_parts", [P, QT, PARTS * N_HEAD], BF16)
        mT = asb("mT", [PARTS * N_HEAD, T], BF16)
        t_mask = SP.dma(mask_f32[:, :, :], mask_rows.rearrange("s n t -> n s t"), c_maskin)
        t_cast = DVE.do(lambda e: e.tensor_copy(mask_bf[:, :, :], mask_f32[:, :, :]), [t_mask])
        t_identb = DVE.do(lambda e: e.tensor_copy(ident_bf[:, :], ident[:, :]), [consts])
        stack_ready = []

        def prepare_stack(i):
            lane = DVE if i == 0 else POOL
            tz = [lane.do(lambda e, i=i: e.memset(stack_mem[i].bitcast(U32), 0), [lane.latest()])]
            for hp in range(2):
                lane.do(lambda e, i=i, hp=hp: e.memset(
                    k_stack[i][HALF * hp:HALF * hp + PARTS, hp, :, :], 1.0), tz + [lane.latest()])
                r = HALF * hp + ROW_MASK
                for s, stack in ((0, q_stack[i][r:r + N_MASK, :, :]), (1, k_stack[i][r:r + N_MASK, hp, :, :])):
                    src = mask_bf[:, s:s + 1, :].broadcast_to([N_MASK, NP, T])
                    SP.dma(stack, src, c_mask[i], [t_cast] + tz)
            stack_ready.append([c_mask[i].all(), (lane.sem, lane.count)])

        prepare_stack(0)
        for v in range(2):
            t_v1 = DVE.do(lambda e: e.memset(v_aug[v][:, :, :, D:D + 1], 1.0))
        DVE.do(lambda e: e.memset(ones[:, :], 1.0))
        t_pv0 = DVE.do(lambda e: e.memset(psum[:, PV_BANK, :], 0.0))
        t_zeros = DVE.do(lambda e: e.memset(zeros[:, :, :], 0.0))
        t_filled = DVE.do(lambda e: e.tensor_copy(filled[:, :], region[:, :]), [consts])
        t_half = DVE.do(lambda e: e.memset(minus_half[:, :], -0.5))
        v_free = [t_v1, t_v1]

        misc_state = {"next": 0, "free": [None] * len(MISC_BANKS)}

        def misc_take():
            n = misc_state["next"]
            misc_state["next"] = (n + 1) % len(MISC_BANKS)
            return n, psum[:, MISC_BANKS[n], :], misc_state["free"][n]

        def misc_free(n, token):
            misc_state["free"][n] = token

        n, bank, free = misc_take()
        PE.do(lambda e: e.transpose(bank[:, 0:NE], rw_row[:, :], ident[0:NE, 0:NE]), [consts], False)
        t = PE.do(lambda e: e.transpose(bank[:, P:P + (NE + 1) * HT], b1_row[:, :],
                                        ident[0:(NE + 1) * HT, 0:(NE + 1) * HT]))
        PE.do(lambda e: e.transpose(bank[:, 2 * P:2 * P + NE + 1], b2_row[:, :], ident[0:NE + 1, 0:NE + 1]))
        DVE.do(lambda e: e.tensor_copy(rwT[:, :], bank[:, 0:NE]), [PE.latest()])
        DVE.do(lambda e: e.tensor_copy(b2T[:, :], bank[:, 2 * P:2 * P + NE + 1]))
        t_wT = DVE.do(lambda e: e.tensor_copy(b1T[:, :], bank[:, P:P + (NE + 1) * HT]))
        misc_free(n, t_wT)

        state = {k: {} for k in ("stored", "loaded", "m_loaded", "x_done", "m_done", "latT", "v",
                                 "outT", "mx_free", "pv", "filled")}
        last = {"rsum": None, "xnT": None, "xT": None, "raw": None, "attn": None, "attnT": None, "outT_free": None,
                "latT": [None] * NSTACK, "parts_free": None, "mT_free": None,
                "m_parts_free": None, "mx_free": [None, None]}

        def project(b):
            n, bank, free = misc_take()
            for j in range(QT):
                t = PE.do(lambda e: e.transpose(bank[:, j * P:(j + 1) * P], x_tok[:, b * QT + j, :],
                                                ident[:, :]),
                          [free, c_x[b].all(), consts] if j == 0 else (), j == QT - 1)
            yield 1
            t_xT = ACTE.do(lambda e: e.activation(xT[0][:, :], bank, ACT.Copy), [t, last["xT"]])
            misc_free(n, t_xT)
            yield 4
            n, bank, free = misc_take()
            t = PE.do(lambda e: e.matmul(bank[0:L, :], wdown_sb[:, :], xT[0][:, :], start=True, stop=True),
                      [free, t_xT])
            yield 1
            t_lat = ACTE.do(lambda e: e.activation(latT[b % NSTACK][:, :], bank[0:L, :], ACT.Copy),
                            [t, last["latT"][b % NSTACK]])
            misc_free(n, t_lat)
            state["latT"][b] = t_lat
            for s in range(2):
                w, src = ((wq_sb[:, :], xT[0][:, :]), (wk_sb[:, :], latT[b % NSTACK][:, :]))[s]
                yield 3
                n, bank, free = misc_take()
                t = PE.do(lambda e: e.matmul(bank, w, src, start=True, stop=True), [free, t_lat, t_xT])
                if s == 0:
                    last["xT"] = t
                yield 1
                t_raw = ACTE.do(lambda e: e.activation(raw[:, :], bank, ACT.Copy,
                                                       scale=SCALE if s == 0 else 1.0), [t, last["raw"]])
                misc_free(n, t_raw)
                yield 4
                n, bank, free = misc_take()
                t = PE.do(lambda e: e.matmul(bank, swap_sb[:, :], raw[:, :], start=True, stop=True),
                          [free, t_raw])
                t_c = POOL.do(lambda e: e.tensor_tensor(raw[:, :], raw[:, :], cos_sb[:, :], ALU.mult), [t])
                yield 1
                t_s = DVE.do(lambda e: e.tensor_tensor(turned[:, :], bank, sin_sb[:, :], ALU.mult),
                             [t, last["raw"]])
                misc_free(n, t_s)
                t_r = POOL.do(lambda e: e.tensor_tensor(turned[:, :], turned[:, :], raw[:, :], ALU.add),
                              [t_c, t_s])
                yield 4
                pt = parts
                t_h = ACTE.do(lambda e: e.activation(pt[:, 0, :], turned[:, :], ACT.Copy),
                              [t_r, last["parts_free"]])
                t_r1 = POOL.do(lambda e: e.tensor_tensor(raw[:, :], turned[:, :], pt[:, 0, :],
                                                         ALU.subtract), [t_h])
                t_m = POOL.do(lambda e: e.tensor_copy(pt[:, 1, :], raw[:, :]), [t_r1])
                t_l = POOL.do(lambda e: e.tensor_tensor(pt[:, 2, :], raw[:, :], pt[:, 1, :],
                                                        ALU.subtract), [t_m])
                last["raw"] = t_l
                last["parts_free"] = SP.dma(scr_qk[b, s], pt[:, :, :], c_store[s], [t_l])
            state["stored"][b] = [c_store[0].all(), c_store[1].all()]

        def load_stacks(b):
            i = b % NSTACK
            gate_ = [state["x_done"].get(b - NSTACK)]
            for hp in range(2):
                t_z = POOL.do(lambda e, hp=hp: e.memset(
                    q_stack[i][HALF * hp:HALF * hp + PARTS, :, :].bitcast(U32), 0),
                    gate_ + stack_ready[i] + [POOL.latest()])
            first = gate_ + stack_ready[i] + state["stored"][b]
            for s in range(2):
                for hp in range(2):
                    src = scr_qk[b, s].rearrange("(j h d) c t -> h c d j t", h=2, d=D)[hp]
                    for n, term in enumerate(TERMS):
                        r = HALF * hp + ROW_TERM + D * n
                        dst = (q_stack[i][r:r + D, :, :] if s == 0 else k_stack[i][r:r + D, hp, :, :])
                        SP.dma(dst, src[term[s]], c_stack[i], first)
            state["loaded"][b] = [c_stack[i].all(), t_z]

        def values(b):
            n, bank, free = misc_take()
            for j in range(QT):
                t = PE.do(lambda e, j=j: e.matmul(bank[:, j * P:(j + 1) * P], latT[b % NSTACK][:, j * P:(j + 1) * P],
                                                  wv_sb[:, :], start=True, stop=True),
                          [free, state["latT"][b]] if j == 0 else (), j == QT - 1)
            last["latT"][b % NSTACK] = t
            yield 1
            t_v = ACTE.do(lambda e: e.activation(
                v_aug[b % 2][:, :, :, 0:D], bank.rearrange("p (q h d) -> p q h d", q=QT, d=D), ACT.Copy),
                [t, v_free[b % 2]])
            misc_free(n, t_v)
            state["v"][b] = t_v

        def place_maxima(b):
            m = mx[b % 2]
            neg = m_parts
            part = lambda c: neg[:, :, c * N_HEAD:(c + 1) * N_HEAD]
            t1 = DVE.do(lambda e: e.tensor_scalar(part(0), m[:, :, :], -1.0, None, ALU.mult),
                        [state["m_done"][b], last["m_parts_free"]])
            t2 = DVE.do(lambda e: e.scalar_tensor_tensor(out=m_rest[:, :, :], in0=m[:, :, :], scalar=-1.0,
                                                         in1=part(0), op0=ALU.mult, op1=ALU.subtract), [t1])
            last["mx_free"][b % 2] = t2
            t3 = DVE.do(lambda e: e.tensor_copy(part(1), m_rest[:, :, :]), [t2])
            t4 = DVE.do(lambda e: e.tensor_tensor(part(2), m_rest[:, :, :], part(1), ALU.subtract), [t3])
            yield 3
            n, bank, free = misc_take()
            bank_bf = bank.bitcast(BF16)
            for j in range(QT):
                t = PE.do(lambda e, j=j: e.transpose(bank_bf[0:PARTS * N_HEAD, j * P:(j + 1) * P],
                                                     neg[:, j, :], ident_bf[:, :]),
                          [free, t4, t_identb] if j == 0 else (), j == QT - 1)
            last["m_parts_free"] = t
            t5 = ACTE.do(lambda e: e.activation(mT[:, :], bank_bf[0:PARTS * N_HEAD, 0:T], ACT.Copy),
                         [t, last["mT_free"]])
            misc_free(n, t5)
            t6 = SP.dma(scr_m[b], mT[:, :], c_mst[b % 2], [t5])
            last["mT_free"] = t6
            for hp in range(2):
                SP.dma(q_stack[b % NSTACK][HALF * hp:HALF * hp + PARTS, :, :],
                       scr_m[b].rearrange("(c j h) t -> h c j t", c=PARTS, h=2)[hp],
                       c_mld[b % NSTACK], [t6, state["m_done"][b]])
            state["m_loaded"][b] = c_mld[b % NSTACK].all()
            yield

        def finish(b):
            tiles = slice(b * QT, (b + 1) * QT)
            attn_row = attn[:, :, :].rearrange("p q (h d) -> p q h d", d=D)
            for j in range(QT):
                n, bank, free = misc_take()
                for g in range(NG):
                    t = PE.do(lambda e: e.transpose(
                        bank[:, g * P:(g + 1) * P], outT[0][:, g, j * P:(j + 1) * P], ident[:, :]),
                        [free, state["outT"][b]] if g == 0 else (), g == NG - 1)
                heads = bank.rearrange("p (h c) -> p h c", c=VW)
                t_rs = DVE.do(lambda e: e.reciprocal(rsum[:, :], heads[:, :, D]),
                              [t, last["rsum"]])
                t_a = DVE.do(lambda e: e.tensor_tensor(
                    attn_row[:, j, :, :], heads[:, :, 0:D],
                    rsum[:, :].unsqueeze(2).broadcast_to([P, N_HEAD, D]), ALU.mult), [t_rs, last["attn"]])
                last["rsum"] = t_a
                misc_free(n, t_a)
                yield 2
            last["outT_free"] = t
            yield 1
            n, bank, free = misc_take()
            for j in range(QT):
                t = PE.do(lambda e: e.transpose(bank[:, j * P:(j + 1) * P], attn[:, j, :], ident[:, :]),
                          [free, t_a] if j == 0 else (), j == QT - 1)
            last["attn"] = t
            t_aT = ACTE.do(lambda e: e.activation(attnT[:, :], bank, ACT.Copy), [t, last["attnT"]])
            misc_free(n, t_aT)
            yield 4
            n, bank, free = misc_take()
            for j in range(QT):
                t = PE.do(lambda e: e.matmul(bank[:, j * P:(j + 1) * P], attnT[:, j * P:(j + 1) * P],
                                             wo_sb[:, :], start=True, stop=True),
                          [free, t_aT] if j == 0 else (), j == QT - 1)
            last["attnT"] = t
            rows = x_tok[:, tiles, :]
            t_y = DVE.do(lambda e: e.tensor_tensor(rows, bank.rearrange("p (q e) -> p q e", q=QT), rows,
                                                   ALU.add), [t])
            misc_free(n, t_y)
            yield 1
            for j in range(QT):
                t_s = DVE.do(lambda e: e.bn_stats(stats[:, j, :], x_tok[:, b * QT + j, :]), [t_y])
            for j in range(QT):
                t_m = DVE.do(lambda e: e.bn_aggr(moments[:, j, :], stats[:, j, :]), [t_s])
            var = moments[:, :, 1]
            POOL.do(lambda e: e.tensor_scalar(rstd[:, :], var, LN_EPS, None, ALU.add), [t_m])
            POOL.do(lambda e: e.tensor_tensor(rstd[:, :], rstd[:, :], minus_half[:, :], ALU.pow), [t_half])
            POOL.do(lambda e: e.tensor_tensor(rms[:, :], rstd[:, :], rstd[:, :], ALU.mult))
            POOL.do(lambda e: e.tensor_tensor(rms[:, :], rms[:, :], var, ALU.mult))
            POOL.do(lambda e: e.tensor_scalar(rms[:, :], rms[:, :], RMS_EPS, None, ALU.add))
            t2 = POOL.do(lambda e: e.tensor_tensor(rms[:, :], rms[:, :], minus_half[:, :], ALU.pow))
            yield 4
            for j in range(QT):
                t_n = DVE.do(lambda e: e.tensor_scalar(
                    x_tok[:, b * QT + j, :], x_tok[:, b * QT + j, :], moments[:, j, 0:1], rstd[:, j:j + 1],
                    ALU.subtract, ALU.mult), [t2], j == QT - 1)
            for j in range(QT):
                t_xn = DVE.do(lambda e: e.scalar_tensor_tensor(
                    out=xn[b % 2][:, j, :], in0=x_tok[:, b * QT + j, :], scalar=rms[:, j:j + 1],
                    in1=nw_rows[:, :], op0=ALU.mult, op1=ALU.mult),
                    [t_n, c_scatter[b % 2].all() if b >= 2 else None], j == QT - 1)
            yield 3
            n, bank, free = misc_take()
            for j in range(QT):
                t = PE.do(lambda e: e.transpose(bank[:, j * P:(j + 1) * P], xn[b % 2][:, j, :], ident[:, :]),
                          [free, t_xn] if j == 0 else (), j == QT - 1)
            flat = lambda a: a[:, tiles, :].rearrange("p q t -> p (q t)")
            t_xnT = ACTE.do(lambda e: e.activation(xnT[:, :], bank, ACT.Copy), [t, last["xnT"]])
            t_hi = ACTE.do(lambda e: e.activation(flat(xnT_hi), bank, ACT.Copy))
            misc_free(n, t_hi)
            POOL.do(lambda e: e.tensor_tensor(flat(xnT_lo), xnT[:, :], flat(xnT_hi).bitcast(F32),
                                              ALU.subtract), [t_hi])
            yield 4
            n, bank, free = misc_take()
            for j in range(QT):
                t = PE.do(lambda e: e.matmul(bank[:, j * NE:(j + 1) * NE], xnT[:, j * P:(j + 1) * P],
                                             rwT[:, :], start=True, stop=True),
                          [free, t_xnT, t_wT] if j == 0 else (), j == QT - 1)
            last["xnT"] = POOL.latest()
            t_e = ACTE.do(lambda e: e.activation(gate[:, :, :].rearrange("p q n -> p (q n)"),
                                                 bank[:, 0:QT * NE], ACT.Exp, scale=-1.0), [t])
            misc_free(n, t_e)
            yield 4
            t1 = DVE.do(lambda e: e.tensor_scalar(gate[:, :, :], gate[:, :, :], 1.0, None, ALU.add), [t_e])
            t2 = DVE.do(lambda e: e.reciprocal(gate[:, :, :], gate[:, :, :]), [t1])
            mine = gate[:, :, :].unsqueeze(3).broadcast_to([P, QT, NE, NE])
            other = gate[:, :, :].unsqueeze(2).broadcast_to([P, QT, NE, NE])
            earlier = before[:, :, :].unsqueeze(1).broadcast_to([P, QT, NE, NE])
            t3 = DVE.do(lambda e: e.tensor_tensor(above[:, :, :, :], other, mine, ALU.is_gt), [t2])
            t4 = DVE.do(lambda e: e.tensor_tensor(equal[:, :, :, :], other, mine, ALU.is_equal))
            t5 = DVE.do(lambda e: e.tensor_tensor(equal[:, :, :, :], equal[:, :, :, :], earlier, ALU.mult), [t4])
            t6 = DVE.do(lambda e: e.tensor_tensor(above[:, :, :, :], above[:, :, :, :], equal[:, :, :, :],
                                                  ALU.add), [t5])
            t7 = DVE.do(lambda e: e.tensor_reduce(rank[:, :, :], above[:, :, :, :], AXIS_X, ALU.add), [t6])
            t8 = DVE.do(lambda e: e.tensor_scalar(chosen[:, :, :], rank[:, :, :], float(TOPK), None,
                                                  ALU.is_lt), [t7])
            yield 3
            n, bank, free = misc_take()
            sel = chosen[:, :, :].rearrange("p q n -> p (q n)")
            PE.do(lambda e: e.matmul(bank[:, 0:QT * NE], prior[:, :], sel, start=True, stop=True),
                  [free, t8], False)
            t = PE.do(lambda e: e.matmul(bank[:, P:P + QT * NE], ones[:, :], sel, start=True, stop=True))
            ahead = bank[:, 0:QT * NE].rearrange("p (q n) -> p q n", n=NE)
            total = bank[:, P:P + QT * NE].rearrange("p (q n) -> p q n", n=NE)
            for k in range(TOPK):
                tw = DVE.do(lambda e: e.scalar_tensor_tensor(
                    out=picked[:, k, :, :], in0=rank[:, :, :], scalar=float(k), in1=gate[:, :, :],
                    op0=ALU.is_equal, op1=ALU.mult), [t7])
            tw = DVE.do(lambda e: e.tensor_reduce(share[:, :, tiles], picked[:, 0:TOPK, :, :], AXIS_X,
                                                  ALU.add), [tw])
            tg = DVE.do(lambda e: e.tensor_tensor(gsum[:, :], share[:, 0, tiles], share[:, 1, tiles],
                                                  ALU.add), [tw])
            tg = DVE.do(lambda e: e.tensor_scalar(gsum[:, :], gsum[:, :], TOPK_EPS, None, ALU.add), [tg])
            tg = DVE.do(lambda e: e.reciprocal(gsum[:, :], gsum[:, :]), [tg])
            DVE.do(lambda e: e.tensor_tensor(share[:, :, tiles], share[:, :, tiles],
                                             gsum[:, :].unsqueeze(1).broadcast_to([P, TOPK, QT]),
                                             ALU.mult), [tg])
            yield 1
            for j in range(QT):
                ta = DVE.do(lambda e: e.tensor_tensor(row_all[:, j, :], ahead[:, j, :], filled[:, :],
                                                      ALU.add), [t, t_filled, state["filled"].get(0)])
                state["filled"][0] = DVE.do(lambda e: e.tensor_tensor(
                    filled[:, :], total[:, j, :], filled[:, :], ALU.add), [ta])
            misc_free(n, state["filled"][0])
            for k in range(TOPK):
                tr = DVE.do(lambda e: e.scalar_tensor_tensor(
                    out=picked[:, TOPK + k, :, :], in0=rank[:, :, :], scalar=float(k),
                    in1=row_all[:, :, :], op0=ALU.is_equal, op1=ALU.mult), [ta])
            tr = DVE.do(lambda e: e.tensor_reduce(row_f[:, :, :], picked[:, TOPK:, :, :], AXIS_X,
                                                  ALU.add), [tr])
            tr = DVE.do(lambda e: e.tensor_copy(row_of[:, :, tiles], row_f[:, :, :]), [tr])
            for j in range(QT):
                for k in range(TOPK):
                    POOL.wait([tr])
                    c = c_scatter[b % 2]
                    c.count += 16
                    nc.gpsimd.indirect_dma_start(
                        xs_dram, bass.IndirectOffsetOnAxis(row_of[:, k, b * QT + j:b * QT + j + 1], 0),
                        xn[b % 2][:, j, :], None).then_inc(c.sem, 16)

        ring = {"exp": 0, "max": 0}
        exp_free = [None] * len(EXP_BANKS)
        max_free = [None] * len(MAX_BANKS)
        probs_free = [None] * NPROB
        pv_free = [t_pv0]
        exp_tok = {}

        def exp_slot(G, s):
            b, g = divmod(G, NG)
            qs, ks = q_stack[b % NSTACK], k_stack[b % NSTACK]
            r = ring["exp"] % len(EXP_BANKS)
            ring["exp"] += 1
            bank = psum[:, EXP_BANKS[r], :]
            if s < GH:
                plan = [(g * GH + s, 0, 0)]
            elif s < 2 * GH:
                plan = [(g * GH + s - GH, 1, 0), (g * GH + s - GH, 3, 3 * P)]
            else:
                plan = [(g * GH + 2 * (s - 2 * GH) + i, 2, 2 * P * i) for i in range(2)]
            for n, (h, kt, at) in enumerate(plan):
                j, hp = divmod(h, 2)
                width = T - kt * P
                t = PE.do(lambda e, j=j, hp=hp, kt=kt, at=at, width=width: e.matmul(
                    bank[:, at:at + width], ks[:, hp, j, kt * P:(kt + 1) * P], qs[:, j, kt * P:T],
                    start=True, stop=True),
                    [exp_free[r], state["m_loaded"][b]] if n == 0 else (), n == len(plan) - 1)
            if s == SLOTS - 1 and g == NG - 1:
                state["x_done"][b] = t
            held = (G * SLOTS + s) % NPROB
            te = ACTE.do(lambda e: e.activation(probs[:, held, :], bank, ACT.Exp),
                         [t, probs_free[held]])
            exp_free[r] = te
            exp_tok[G, s] = te

        def pv(G, kt):
            b, g = divmod(G, NG)
            at = {0: (0, 0), 1: (GH, 0), 3: (GH, 3 * P)}
            need = [exp_tok[G, {0: GH - 1, 1: 2 * GH - 1, 3: 2 * GH - 1, 2: SLOTS - 1}[kt]]]
            if kt == 0:
                need += [pv_free[0], state["v"][b]]
            for i in range(GH):
                h = g * GH + i
                width = T - kt * P
                s, c = (2 * GH + i // 2, 2 * P * (i % 2)) if kt == 2 else (at[kt][0] + i, at[kt][1])
                t = PE.do(lambda e, i=i, h=h, s=s, c=c, width=width: e.matmul(
                    psum[VW * i:VW * i + D + 1, PV_BANK, kt * P:T], v_aug[b % 2][:, kt, h, :],
                    probs[:, (G * SLOTS + s) % NPROB, c:c + width], start=(kt == 0), stop=(kt == 2),
                    skip_group_check=True, tile_position=(0, VW * i)), need if i == 0 else (), i == GH - 1)
            done = {0: range(GH), 1: (), 3: range(GH, 2 * GH), 2: range(2 * GH, SLOTS)}[kt]
            for s in done:
                probs_free[(G * SLOTS + s) % NPROB] = t
            if kt == 2:
                state["pv"][G] = t
                if g == NG - 1:
                    v_free[b % 2] = t

        def pv_out(G):
            b, g = divmod(G, NG)
            t = ACTE.do(lambda e: e.activation(outT[0][:, g, :], psum[:, PV_BANK, :], ACT.Copy),
                        [state["pv"][G], last["outT_free"]])
            pv_free[0] = t
            state["outT"][b] = t

        def max_slot(G, s):
            b, g = divmod(G, NG)
            qs, ks = q_stack[b % NSTACK], k_stack[b % NSTACK]
            r = ring["max"] % len(MAX_BANKS)
            ring["max"] += 1
            bank = psum[:, MAX_BANKS[r], :]
            if s < GH:
                plan = [(g * GH + s, 3, 0)]
            elif s < 2 * GH:
                plan = [(g * GH + s - GH, 2, 0), (g * GH + s - GH, 0, 3 * P)]
            else:
                plan = [(g * GH + 2 * (s - 2 * GH) + i, 1, 2 * P * i) for i in range(2)]
            for n, (h, qt, at) in enumerate(plan):
                j, hp = divmod(h, 2)
                width = (qt + 1) * P
                t = PE.do(lambda e, j=j, hp=hp, qt=qt, at=at, width=width: e.matmul(
                    bank[:, at:at + width], qs[:, j, qt * P:(qt + 1) * P], ks[:, hp, j, 0:width],
                    start=True, stop=True),
                    [max_free[r]] + state["loaded"][b] if n == 0 else (), n == len(plan) - 1)
            m = mx[b % 2]
            need = [t, last["mx_free"][b % 2]]
            if s < 2 * GH:
                for h, qt, at in plan:
                    width = (qt + 1) * P
                    t = DVE.do(lambda e, h=h, qt=qt, at=at, width=width: e.tensor_reduce(
                        m[:, qt, h:h + 1], bank[:, at:at + width], AXIS_X, ALU.max), need)
            else:
                h = plan[0][0]
                t = DVE.do(lambda e: e.tensor_reduce(
                    m[:, 1, h:h + 2], bank.rearrange("p (h k) -> p h k", h=2), AXIS_X, ALU.max), need)
            max_free[r] = t
            if s == SLOTS - 1 and g == NG - 1:
                state["m_done"][b] = t

        background, clock = [], [0]

        def advance():
            clock[0] += 1
            steps = 0
            for job in list(background):
                if job[1] > clock[0] or steps == 2:
                    continue
                steps += 1
                wait = next(job[0], None)
                if wait is None:
                    background.remove(job)
                else:
                    job[1] = clock[0] + wait

        def start(work, first=False):
            background.insert(0 if first else len(background), [work, clock[0]])

        def run_all():
            while background:
                advance()

        start(project(0))
        run_all()
        load_stacks(0)
        for i in range(1, NSTACK):
            prepare_stack(i)
        for idx in range(-LEAD, B * NG + 1):
            X, M = idx, idx + LEAD
            b, g = divmod(idx, NG)
            if g == 2 and 0 <= b + 1 < B:
                start(place_maxima(b + 1), first=True)
                advance()
            if g == 3 and 0 <= b + 1 < B:
                start(values(b + 1))
            if g == 0 and 0 < b + 2 < B:
                run_all()
                load_stacks(b + 2)
            if g == 0 and b - 1 == B - NSTACK:
                load_weights(range(FIRST_FFNS), [state["x_done"][b - 1]])
            if g == 0 and b - 1 == B - NSTACK + 1:
                load_weights(range(FIRST_FFNS, NE + 1), [state["x_done"][b - 1]])
            if idx == -LEAD:
                start(project(1))
            if g == 1 and 2 < b + 3 < B or idx == -3:
                start(project(max(b + 3, 2)))
            for s in range(SLOTS):
                if 0 <= X < B * NG:
                    if s == 0 and g == 0:
                        run_all()
                    exp_slot(X, s)
                if 0 <= M < B * NG:
                    max_slot(M, s)
                if s == 6 and 0 <= X < B * NG:
                    pv(X, 0)
                if s == 9 and 0 <= X < B * NG:
                    pv(X, 1)
                if s == 0 and 1 <= X <= B * NG:
                    pv(X - 1, 3)
                if s == 1 and 1 <= X <= B * NG:
                    pv(X - 1, 2)
                if s == 3 and 1 <= X <= B * NG:
                    pv_out(X - 1)
                    if g == 0:
                        start(finish(b - 1))
                advance()

        att_end = [ln.latest() for ln in (PE, ACTE, DVE, POOL)]
        att.close()

        def fsb(name, shape, dt=F32, side="left"):
            return ctx.enter_context(nc.sbuf_tensor(name, shape, dt, side=side))

        H2 = H // 2
        w_split = fsb("w_split", [P, NE + 1, 2, 2, H], F32R)
        x_in = [fsb(f"x_in{i}", [P, 2, E]) for i in range(3)]
        y_out = [fsb(f"y_out{i}", [P, 2, E]) for i in range(3)]
        n_tiles = fsb("n_tiles", [P, NE])
        over = fsb("over", [P, NE, MAX_E_TILES])
        cum_all = fsb("cum_all", [P, NE, NE])
        cum = fsb("cum", [P, NE])
        passed, passed_n = (a[:, 0:N_TILES * NE].rearrange("p (t n) -> p t n", n=NE) for a in (xnT, attnT))
        t_expert = fsb("t_expert", [P, N_TILES])
        t_before = fsb("t_before", [P, N_TILES])
        t_row = fsb("t_row", [P, N_TILES])
        table = fsb("table", [P, 2, N_TILES], U32)
        delta = fsb("delta", [P, NE])
        step_ = fsb("step", [P, NE])
        shift = fsb("shift", [P, TOPK * NT])
        row_y = fsb("row_y", [P, TOPK, NT], U32)
        inside = attn[:, :, :].rearrange("p q (a n) -> p (q a) n", n=NE)
        region_end = fsb("region_end", [P, NE], U32)
        f_stats = fsb("f_stats", [P, 2, 6])
        f_moments = [fsb(f"f_moments{i}", [P, 2, 2]) for i in range(2)]
        f_rstd = [fsb(f"f_rstd{i}", [P, 2]) for i in range(2)]

        split_done = {}

        def split_weights():
            weights = c_w.all()
            for f in list(range(1, NE + 1)) + [0]:
                raw_w = w_sb[:, f, :].rearrange("p (w h) -> p w h", w=2)
                th = ACTE.do(lambda e: e.activation(w_split[:, f, :, 0, :], raw_w, ACT.Copy),
                             [weights] + att_end)
                lane = DVE if f % 2 else POOL
                split_done[f] = lane.do(lambda e: e.tensor_tensor(
                    w_split[:, f, :, 1, :], raw_w, w_split[:, f, :, 0, :].bitcast(F32), ALU.subtract),
                    [th] + att_end)
                yield 1

        start(split_weights())
        run_all()

        t = DVE.do(lambda e: e.tensor_copy(region_end[:, :], filled[:, :]),
                   [ln.latest() for ln in (PE, ACTE, DVE, POOL)])
        t_end = t
        t = DVE.do(lambda e: e.tensor_tensor(cum[:, :], filled[:, :], region[:, :], ALU.subtract))
        t = DVE.do(lambda e: e.tensor_tensor(over[:, :, :], cum[:, :].unsqueeze(2).broadcast_to(
            [P, NE, MAX_E_TILES]), thresholds[:, :, :], ALU.is_gt), [t])
        t = DVE.do(lambda e: e.tensor_reduce(n_tiles[:, :], over[:, :, :], AXIS_X, ALU.add), [t])
        t = DVE.do(lambda e: e.tensor_tensor(cum_all[:, :, :], n_tiles[:, :].unsqueeze(1).broadcast_to(
            [P, NE, NE]), upto[:, :, :], ALU.mult), [t])
        t = DVE.do(lambda e: e.tensor_reduce(cum[:, :], cum_all[:, :, :], AXIS_X, ALU.add), [t])
        per_tile = lambda a: a[:, :].unsqueeze(1).broadcast_to([P, N_TILES, NE])
        t = DVE.do(lambda e: e.tensor_tensor(passed[:, :, :], tile_index[:, :, :], per_tile(cum),
                                             ALU.is_ge), [t])
        t = DVE.do(lambda e: e.tensor_tensor(passed_n[:, :, :], passed[:, :, :], per_tile(n_tiles),
                                             ALU.mult), [t])
        t = DVE.do(lambda e: e.tensor_reduce(t_before[:, :], passed_n[:, :, :], AXIS_X, ALU.add), [t])
        t = DVE.do(lambda e: e.tensor_reduce(t_expert[:, :], passed[:, :, :], AXIS_X, ALU.add), [t])
        t = DVE.do(lambda e: e.tensor_tensor(t_before[:, :], tile_index[:, :, 0], t_before[:, :],
                                             ALU.subtract), [t])
        t = DVE.do(lambda e: e.tensor_scalar(t_row[:, :], t_expert[:, :], float(ROWS), None, ALU.mult), [t])
        t = DVE.do(lambda e: e.scalar_tensor_tensor(out=t_row[:, :], in0=t_before[:, :], scalar=float(FT),
                                                    in1=t_row[:, :], op0=ALU.mult, op1=ALU.add), [t])
        DVE.do(lambda e: e.tensor_scalar(table[:, 0, :], t_expert[:, :], float(NE - 1), None, ALU.min), [t])
        t_table = DVE.do(lambda e: e.tensor_scalar(table[:, 1, :], t_row[:, :], float(NE * ROWS), None,
                                                   ALU.min), [t])

        t = DVE.do(lambda e: e.tensor_tensor(delta[:, :], cum[:, :], n_tiles[:, :], ALU.subtract), [t])
        t = DVE.do(lambda e: e.scalar_tensor_tensor(out=delta[:, :], in0=delta[:, :], scalar=float(FT),
                                                    in1=region[:, :], op0=ALU.mult, op1=ALU.subtract), [t])
        t = DVE.do(lambda e: e.tensor_copy(step_[:, :], delta[:, :]), [t])
        t = DVE.do(lambda e: e.tensor_tensor(step_[:, 1:], delta[:, 1:], delta[:, 0:NE - 1],
                                             ALU.subtract), [t])
        rows_x = row_of[:, :, :].rearrange("p k t -> p (k t)")
        each = lambda a: a[:, :].unsqueeze(1).broadcast_to([P, TOPK * NT, NE])
        t = DVE.do(lambda e: e.tensor_tensor(inside, rows_x.unsqueeze(2).broadcast_to([P, TOPK * NT, NE]),
                                             each(region), ALU.is_ge), [t])
        t = DVE.do(lambda e: e.tensor_tensor(inside, inside, each(step_), ALU.mult), [t])
        t = DVE.do(lambda e: e.tensor_reduce(shift[:, :], inside, AXIS_X, ALU.add), [t])
        t_row_y = DVE.do(lambda e: e.tensor_tensor(row_y[:, :, :].rearrange("p k t -> p (k t)"), rows_x,
                                                   shift[:, :], ALU.add), [t])

        rows_of = lambda dram, first: dram[bass.ds(first, FT), :].rearrange("(j p) e -> p j e", p=P)
        SP.dma(rows_of(xs_dram, NE * ROWS), zeros[:, :, :], c_zero, [t_zeros])
        SP.wait([t_end])
        for e_ in range(NE):
            first = nc.sync.value_load(region_end[0:1, e_:e_ + 1], min_val=0, max_val=NE * ROWS - FT)
            SP.dma(rows_of(xs_dram, first), zeros[:, :, :], c_zero)
        xs_ready = [c_zero.all()] + [c.all() for c in c_scatter]
        ffn_free = [ln.latest() for ln in (PE, ACTE, DVE, POOL)]
        rec.close()

        g_f = [fsb(f"g_f{i}", [P, HT, FT], side="right") for i in range(2)]
        g_hi = [fsb(f"g_hi{i}", [P, HT, FT], F32R, side="right") for i in range(2)]
        g_lo = [fsb(f"g_lo{i}", [P, HT, FT], F32R, side="right") for i in range(2)]
        x_hi = [fsb(f"x_hi{i}", [P, FT], F32R, side="right") for i in range(2)]
        x_lo = [fsb(f"x_lo{i}", [P, FT], F32R, side="right") for i in range(2)]
        yT = [fsb(f"yT{i}", [P, FT], side="right") for i in range(2)]
        w1_cur = [fsb(f"w1_cur{i}", [P, 2, H], F32R, side="right") for i in range(2)]
        w2_cur = [fsb(f"w2_cur{i}", [P, 2, H], F32R, side="right") for i in range(2)]
        gathered = [outT[0][:, i // 2, (i % 2) * FT:(i % 2 + 1) * FT].rearrange("p (k e) -> p k e", k=TOPK)
                    for i in range(NGATHER)]
        IN_BANKS, HID_BANKS, OUT_BANKS = (0, 1), (2, 3, 4, 5), (6, 7)
        N_SHARED = NT // 2
        N_UNITS = N_TILES + N_SHARED
        unit = [dict() for _ in range(N_UNITS)]
        F0 = [0]

        def bank_of(ring_, n):
            return psum[:, ring_[n % len(ring_)], :]

        def tok(u, name):
            return unit[u].get(name) if 0 <= u < N_UNITS else None

        def fetch(u):
            SP.wait([t_table])
            row = nc.sync.value_load(table[0:1, 1, u:u + 1], min_val=0, max_val=NE * ROWS)
            unit[u]["x_in"] = SP.dma(x_in[u % 3][:, :, :], rows_of(xs_dram, row), c_xs[u % 3],
                                     xs_ready + ffn_free + [tok(u - 3, "turned")])

        def turn_in(u):
            bank = bank_of(IN_BANKS, u)
            for j in range(2):
                t = PE.do(lambda e: e.transpose(bank[:, j * P:(j + 1) * P], x_in[u % 3][:, j, :], ident[:, :]),
                          [unit[u]["x_in"], tok(u - 2, "x_lo")] + ffn_free if j == 0 else (), j == 1)
            unit[u]["turned"] = t
            unit[u]["x_hi"] = ACTE.do(lambda e: e.activation(x_hi[u % 2][:, :], bank[:, 0:FT], ACT.Copy),
                                      [t, tok(u - 2, "hid")])

        def split_in(u):
            unit[u]["x_lo"] = DVE.do(lambda e: e.tensor_tensor(
                x_lo[u % 2][:, :], bank_of(IN_BANKS, u)[:, 0:FT], x_hi[u % 2][:, :].bitcast(F32),
                ALU.subtract), [unit[u]["x_hi"], tok(u - 2, "hid")])

        def take_w1(u):
            DVE.wait([t_table] + ffn_free)
            e_ = nc.vector.value_load(table[0:1, 0, u:u + 1], min_val=0, max_val=NE - 1)
            unit[u]["e_dve"] = e_
            unit[u]["w1"] = DVE.do(lambda e: e.tensor_copy(
                w1_cur[u % 2][:, :, :], w_split[:, bass.ds(e_ + 1, 1), 0, :, :].squeeze(1)),
                [tok(u - 2, "hid")] + list(split_done.values()))

        def take_w2(u):
            e_ = unit[u]["e_dve"]
            unit[u]["w2"] = DVE.do(lambda e: e.tensor_copy(
                w2_cur[u % 2][:, :, :], w_split[:, bass.ds(e_ + 1, 1), 1, :, :].squeeze(1)),
                [tok(u - 2, "out")])

        def hidden(u):
            routed = u < N_TILES
            if routed:
                xh, xl, w = x_hi[u % 2][:, :], x_lo[u % 2][:, :], w1_cur[u % 2]
                need = [unit[u]["x_lo"], unit[u]["w1"]]
            else:
                two = slice(2 * (u - N_TILES), 2 * (u - N_TILES) + 2)
                xh = xnT_hi[:, two, :].rearrange("p q t -> p (q t)")
                xl = xnT_lo[:, two, :].rearrange("p q t -> p (q t)")
                w = w_split[:, 0, 0, :, :]
                need = ffn_free + [split_done[0]]
            for i in range(2):
                bank = bank_of(HID_BANKS, 2 * u + i)
                for c in range(2):
                    t4 = 2 * i + c
                    at = slice(t4 * P, (t4 + 1) * P)
                    dst = bank[:, c * FT:(c + 1) * FT]
                    for n, (wp, xp) in enumerate(((0, xh), (0, xl), (1, xh))):
                        t = PE.do(lambda e: e.matmul(dst, w[:, wp, at], xp, start=(n == 0), stop=(n == 2)),
                                  need + [tok(u - 2, f"g{i}")] if c == 0 and n == 0 else (),
                                  c == 1 and n == 2)
                unit[u][f"hid{i}"] = t
            unit[u]["hid"] = t

        def act(u):
            routed = u < N_TILES
            if routed:
                ACTE.wait([t_table])
                e_ = nc.scalar.value_load(table[0:1, 0, u:u + 1], min_val=0, max_val=NE - 1)
                unit[u]["e_act"] = e_
            for t4 in range(HT):
                i, c = divmod(t4, 2)
                bank = bank_of(HID_BANKS, 2 * u + i)
                bias = b1T[:, bass.ds((e_ + 1) * HT + t4, 1)] if routed else b1T[:, t4:t4 + 1]
                t = ACTE.do(lambda e: e.activation(g_f[u % 2][:, t4, :], bank[:, c * FT:(c + 1) * FT],
                                                   ACT.Relu, bias=bias),
                            [unit[u][f"hid{i}"], tok(u - 2, "g_lo")] if c == 0 else (), c == 1)
                if c == 1:
                    unit[u][f"g{i}"] = t

        def split_act(u):
            routed = u < N_TILES
            th = DVE.do(lambda e: e.tensor_copy(g_hi[u % 2][:, :, :], g_f[u % 2][:, :, :]),
                        [unit[u]["g1"], tok(u - 2, "out")])
            lane = POOL if routed else DVE
            unit[u]["g_lo"] = lane.do(lambda e: e.tensor_tensor(
                g_lo[u % 2][:, :, :], g_f[u % 2][:, :, :], g_hi[u % 2][:, :, :].bitcast(F32),
                ALU.subtract), [th, tok(u - 2, "out")])

        def project_out(u):
            routed = u < N_TILES
            bank = bank_of(OUT_BANKS, u)
            w = w2_cur[u % 2] if routed else w_split[:, 0, 1, :, :]
            need = [unit[u]["g_lo"], unit[u].get("w2"), tok(u - 2, "y")]
            n = 0
            for t4 in range(HT):
                at = slice(t4 * P, (t4 + 1) * P)
                for wp, g in ((0, g_hi), (0, g_lo), (1, g_hi)):
                    t = PE.do(lambda e: e.matmul(bank[:, 0:FT], w[:, wp, at], g[u % 2][:, t4, :],
                                                 start=(n == 0), stop=(n == 3 * HT - 1)),
                              need if n == 0 else (), n == 3 * HT - 1)
                    n += 1
            unit[u]["out"] = t
            bias = b2T[:, bass.ds(unit[u]["e_act"] + 1, 1)] if routed else b2T[:, 0:1]
            unit[u]["yT"] = ACTE.do(lambda e: e.activation(yT[u % 2][:, :], bank[:, 0:FT], ACT.Identity,
                                                           bias=bias), [t, tok(u - 2, "y_turned")])

        def turn_out(u):
            routed = u < N_TILES
            bank = bank_of(OUT_BANKS, u)
            for j in range(2):
                t = PE.do(lambda e: e.transpose(bank[:, FT + j * P:FT + (j + 1) * P],
                                                yT[u % 2][:, j * P:(j + 1) * P], ident[:, :]),
                          [unit[u]["yT"]] if j == 0 else (), j == 1)
            unit[u]["y_turned"] = t
            y = bank[:, FT:2 * FT].rearrange("p (j e) -> p j e", j=2)
            if routed:
                unit[u]["y"] = DVE.do(lambda e: e.tensor_copy(y_out[u % 3][:, :, :], y),
                                      [t, tok(u - 3, "stored")])
                unit[u]["stored"] = SP.dma(rows_of(ys_dram, u * FT), y_out[u % 3][:, :, :], c_ys[u % 3],
                                           [unit[u]["y"]])
            else:
                pair = slice(2 * (u - N_TILES), 2 * (u - N_TILES) + 2)
                unit[u]["y"] = DVE.do(lambda e: e.tensor_tensor(x_tok[:, pair, :], y, x_tok[:, pair, :],
                                                                ALU.add), [t])

        gather_done = {}
        gather_free = [None] * NGATHER

        def gather(i):
            n = i % NGATHER
            POOL.wait([t_row_y, gather_free[n]] + [c.all() for c in c_ys])
            for k in range(TOPK):
                c_gather[n].count += 16
                nc.gpsimd.indirect_dma_start(
                    gathered[n][:, k, :], None, ys_dram,
                    bass.IndirectOffsetOnAxis(row_y[:, k, i:i + 1], 0)).then_inc(c_gather[n].sem, 16)
            gather_done[i] = c_gather[n].all()

        def combine(m):
            for i in (2 * m, 2 * m + 1):
                for k in range(TOPK):
                    t = DVE.do(lambda e: e.scalar_tensor_tensor(
                        out=x_tok[:, i, :], in0=gathered[i % NGATHER][:, k, :],
                        scalar=share[:, k, i:i + 1], in1=x_tok[:, i, :], op0=ALU.mult, op1=ALU.add),
                        [gather_done[i], unit[N_TILES + m]["y"]] if k == 0 else [t])
                gather_free[i % NGATHER] = t
                if i + NGATHER < NT:
                    gather(i + NGATHER)
                t = DVE.do(lambda e: e.bn_stats(f_stats[:, i % 2, :], x_tok[:, i, :]), [t])
                t = DVE.do(lambda e: e.bn_aggr(f_moments[m % 2][:, i % 2, :], f_stats[:, i % 2, :]), [t])
            POOL.do(lambda e: e.tensor_scalar(f_rstd[m % 2][:, :], f_moments[m % 2][:, :, 1], LN_EPS, None,
                                              ALU.add), [t])
            unit[N_TILES + m]["rstd"] = POOL.do(lambda e: e.tensor_tensor(
                f_rstd[m % 2][:, :], f_rstd[m % 2][:, :], minus_half[:, 0:2], ALU.pow))

        def write_out(m):
            for i in (2 * m, 2 * m + 1):
                t = DVE.do(lambda e: e.tensor_scalar(
                    x_tok[:, i, :], x_tok[:, i, :], f_moments[m % 2][:, i % 2, 0:1],
                    f_rstd[m % 2][:, i % 2:i % 2 + 1], ALU.subtract, ALU.mult),
                    [unit[N_TILES + m]["rstd"]])
            SP.dma(out.rearrange("b (q p) e -> p (b q) e", p=P)[:, 2 * m:2 * m + 2, :],
                   x_tok[:, 2 * m:2 * m + 2, :], c_out[0], [t])

        for u in range(3):
            fetch(u)
        for i in range(-1, N_UNITS + 6):
            if 3 <= i + 3 < N_TILES:
                fetch(i + 3)
            if 0 <= i + 1 < N_TILES:
                turn_in(i + 1)
                take_w1(i + 1)
            if 0 <= i < N_UNITS:
                hidden(i)
                act(i)
            if 0 <= i - 1 < N_UNITS:
                split_act(i - 1)
            if 0 <= i + 1 < N_TILES:
                split_in(i + 1)
            if 0 <= i - 3 < N_UNITS:
                turn_out(i - 3)
            if 0 <= i - 2 < N_UNITS:
                project_out(i - 2)
            if 0 <= i - 1 < N_TILES:
                take_w2(i - 1)
            if i - 3 == N_TILES - 1:
                for n in range(NGATHER):
                    gather(n)
            if 0 <= i - 4 - N_TILES < N_SHARED:
                combine(i - 4 - N_TILES)
            if 0 <= i - 5 - N_TILES < N_SHARED:
                write_out(i - 5 - N_TILES)
        SP.wait([c.all() for c in c_out + c_ys])


_INS = ["L0_attn_x", "L0_attn_wq", "L0_attn_w_down", "L0_attn_wk_up", "L0_attn_wv_up", "L0_attn_wo",
        "L0_ffn_norm_weight", "L0_ffn_router_w", "L0_ffn_sw1", "L0_ffn_sb1", "L0_ffn_sw2", "L0_ffn_sb2",
        "L0_ffn_ew1", "L0_ffn_eb1", "L0_ffn_ew2", "L0_ffn_eb2"]


def shape_constants(T, E, n_expert, n_token):
    D = E // N_HEAD
    inv = 1.0 / ROPE_THETA ** (np.arange(0, D, 2, dtype=np.float32) / D)
    ang = np.outer(np.arange(T, dtype=np.float32), inv)
    cos, sin = np.cos(ang).astype(np.float32), np.sin(ang).astype(np.float32)
    pair = (np.arange(E) % D) // 2
    sign = np.where(np.arange(E) % 2 == 0, -1.0, 1.0).astype(np.float32)
    rope_cos = np.ascontiguousarray(cos[:, pair].T)
    rope_sin = np.ascontiguousarray((sin[:, pair] * sign).T)
    swap = np.zeros((E, E), np.float32)
    swap[np.arange(E) ^ 1, np.arange(E)] = 1.0
    t = np.arange(T)
    mask_q, mask_k = [], []
    for tile in range(T // P):
        for page in range(1, P // PAGE):
            start = tile * P
            mask_q.append(np.where((t >= start) & (t < start + page * PAGE), MASK_BIG, 0.0))
            mask_k.append(((t >= start + page * PAGE) & (t < start + (page + 1) * PAGE)) * 1.0)
    mask = np.stack([np.stack(mask_q), np.stack(mask_k)]).astype(np.float32)
    e = np.arange(n_expert)
    n_rows = n_token + 2 * P
    wide = lambda a: np.ascontiguousarray(np.broadcast_to(a.astype(np.float32), (P,) + a.shape))
    prior = np.triu(np.ones((P, P), np.float32), 1)
    n_tiles = n_token * TOPK // (2 * P) + n_expert - 1
    thresholds = np.broadcast_to(2 * P * np.arange(n_token // (2 * P)), (n_expert, n_token // (2 * P)))
    tile_index = np.broadcast_to(np.arange(n_tiles)[:, None], (n_tiles, n_expert))
    return [rope_cos, rope_sin, swap, mask, np.eye(P, dtype=np.float32), wide(e[None, :] < e[:, None]),
            prior, wide(e * n_rows), wide(thresholds), wide(e[None, :] <= e[:, None]), wide(tile_index)]


def kernel(**inputs):
    import numpy as _np
    import concourse.bacc as _bacc
    from concourse import mybir as _mybir
    from concourse.bass_utils import run_bass_kernel_spmd as _run

    nc = _bacc.Bacc("TRN2", target_bir_lowering=False, num_devices=1)
    arrays, args = {}, []

    def give(name, a):
        a = _np.ascontiguousarray(a)
        arrays[name] = a
        args.append(nc.dram_tensor(name, a.shape, _mybir.dt.from_np(a.dtype), kind="ExternalInput").ap())

    for name in _INS:
        give(f"in_{name}", inputs[name])
    B, T, E = inputs["L0_attn_x"].shape
    for i, a in enumerate(shape_constants(T, E, inputs["L0_ffn_ew1"].shape[0], B * T)):
        give(f"const_{i}", a)
    args.append(nc.dram_tensor("out", (B, T, E), F32, kind="ExternalOutput").ap())
    build(nc, *args)
    r = _run(nc, [arrays], core_ids=[0])
    return r.results[0]["out"]
```

```python
from contextlib import ExitStack

import numpy as np
import concourse.bass as bass
from concourse import mybir

F32 = mybir.dt.float32
BF16 = mybir.dt.bfloat16
F32R = mybir.dt.float32r
U32 = mybir.dt.uint32
ACT = mybir.ActivationFunctionType
ALU = mybir.AluOpType
AXIS_X = mybir.AxisListType.X

P = 128
N_HEAD = 16
PAGE = 32
ROPE_THETA = 10000.0
TOPK = 2
LN_EPS = 1e-5
RMS_EPS = 1e-8
TOPK_EPS = 1e-6

HALF = 64
PARTS = 3
TERMS = [(0, 0), (0, 1), (1, 0), (1, 1), (0, 2), (2, 0)]
MASK_BIG = -1.0e38


class Lane:

    def __init__(self, engine, sem, serial=False):
        self.serial = serial
        self.engine, self.sem, self.count, self.seen = engine, sem, 0, {}

    def wait(self, tokens):
        for t in tokens:
            if t is None:
                continue
            sem, value = t
            if self.seen.get(sem.name, 0) < value:
                self.seen[sem.name] = value
                self.engine.wait_ge(sem, value)

    def do(self, make, after=(), signal=True):
        self.wait(after)
        if self.serial:
            self.wait([self.latest()])
        ins = make(self.engine)
        if not signal:
            return None
        self.count += 1
        ins.then_inc(self.sem, 1)
        return (self.sem, self.count)

    def latest(self):
        return (self.sem, self.count)

    def dma(self, out, src, counter, after=()):
        self.wait(after)
        counter.count += 16
        self.engine.dma_start(out, src).then_inc(counter.sem, 16)
        return (counter.sem, counter.count)


class Counter:

    def __init__(self, sem):
        self.sem, self.count = sem, 0

    def all(self):
        return (self.sem, self.count)


def build(nc, x, wq, w_down, wk_up, wv_up, wo, norm_weight, router_w, sw1, sb1, sw2, sb2,
          ew1, eb1, ew2, eb2, rope_cos, rope_sin, rope_swap, mask_rows, ident_in,
          before_in, prior_in, region_in, thresholds_in, upto_in, tile_index_in, out):
    B, T, E = x.shape
    L = w_down.shape[1]
    D = E // N_HEAD
    NE, _, H = ew1.shape
    assert E == P and D == 8 and T == 512
    QT = T // P
    NT = B * QT
    HT = H // P
    NP = N_HEAD // 2
    GH = 4
    NG = N_HEAD // GH
    PPB = P // PAGE
    N_MASK = QT * (PPB - 1)
    ROW_TERM = PARTS
    ROW_MASK = ROW_TERM + D * len(TERMS)
    assert ROW_MASK + N_MASK <= HALF
    SCALE = 1.0 / float(np.sqrt(D))
    VW = 32
    SLOTS = 10
    LEAD = 6
    NSTACK = 3
    FT = 2 * P
    ROWS = NT * P + FT
    N_TILES = NT * P * TOPK // FT + NE - 1
    MAX_E_TILES = NT * P // FT
    NPROB = 12

    ctx = ExitStack()
    with ctx:
        def sb(name, shape, dt=F32):
            return ctx.enter_context(nc.sbuf_tensor(name, shape, dt))

        def sem(name):
            return ctx.enter_context(nc.semaphore(name))

        psum = ctx.enter_context(nc.psum_tensor("psum", [P, 8, 512], F32))
        EXP_BANKS, MAX_BANKS, PV_BANK, MISC_BANKS = (0, 1), (3, 4, 2), 5, (6, 7)

        x_tok = sb("x_tok", [P, NT, E])
        ident = sb("ident", [P, P])
        ident_bf = sb("ident_bf", [P, P], BF16)
        wq_sb, wo_sb = sb("wq_sb", [P, E]), sb("wo_sb", [P, E])
        wdown_sb = sb("wdown_sb", [P, L])
        wk_sb, wv_sb = sb("wk_sb", [L, E]), sb("wv_sb", [L, E])
        nw_rows = sb("nw_rows", [P, E])
        rw_row = sb("rw_row", [NE, E])
        rwT = sb("rwT", [P, NE])
        b1_row = sb("b1_row", [(NE + 1) * HT, P])
        b1T = sb("b1T", [P, (NE + 1) * HT])
        b2_row = sb("b2_row", [NE + 1, P])
        b2T = sb("b2T", [P, NE + 1])
        prior = sb("prior", [P, P])
        ones = sb("ones", [P, P])
        zeros = sb("zeros", [P, FT // P, E])
        region = sb("region", [P, NE])
        filled = sb("filled", [P, NE])
        thresholds = sb("thresholds", [P, NE, MAX_E_TILES])
        upto = sb("upto", [P, NE, NE])
        tile_index = sb("tile_index", [P, N_TILES, NE])
        row_of = sb("row_of", [P, TOPK, NT], U32)
        share = sb("share", [P, TOPK, NT])
        before = sb("before", [P, NE, NE])
        minus_half = sb("minus_half", [P, QT])
        W = H + HT * E
        Q_WORDS, K_WORDS = NP * T // 2, 2 * NP * T // 2
        S_WORDS = Q_WORDS + K_WORDS
        rec = ExitStack()
        recycled = rec.enter_context(nc.sbuf_tensor("recycled", [P, 2 * S_WORDS], F32, side="right"))
        w_sb = recycled[:, 0:(NE + 1) * W].rearrange("p (f w) -> p f w", w=W)
        FIRST_FFNS = S_WORDS // W
        xnT_hi = sb("xnT_hi", [P, NT, P], F32R)
        xnT_lo = sb("xnT_lo", [P, NT, P], F32R)

        outT = [sb("outT0", [P, NG, T])]
        rsum = sb("rsum", [P, N_HEAD])
        attn = sb("attn", [P, QT, E])
        attnT = sb("attnT", [P, T])
        stats = sb("stats", [P, QT, 6])
        moments = sb("moments", [P, QT, 2])
        rstd = sb("rstd", [P, QT])
        rms = sb("rms", [P, QT])
        xn = [sb(f"xn{i}", [P, QT, E]) for i in range(2)]
        xnT = sb("xnT", [P, T])
        gate = sb("gate", [P, QT, NE])
        above = sb("above", [P, QT, NE, NE])
        equal = sb("equal", [P, QT, NE, NE])
        rank = sb("rank", [P, QT, NE])
        chosen = sb("chosen", [P, QT, NE])
        row_all = sb("row_all", [P, QT, NE])
        picked = sb("picked", [P, 2 * TOPK, QT, NE])
        row_f = sb("row_f", [P, TOPK, QT])
        gsum = sb("gsum", [P, QT])

        att = ExitStack()

        def asb(name, shape, dt=F32):
            return att.enter_context(nc.sbuf_tensor(name, shape, dt))

        cos_sb, sin_sb = asb("cos_sb", [P, T]), asb("sin_sb", [P, T])
        swap_sb = asb("swap_sb", [P, P])

        PE, ACTE, DVE, POOL, SP = (Lane(e, sem(n), n == "pool") for n, e in (
            ("pe", nc.tensor), ("act", nc.scalar), ("dve", nc.vector), ("pool", nc.gpsimd),
            ("sp", nc.sync)))
        c_const, c_late = Counter(sem("c_const")), Counter(sem("c_late"))
        c_x = [Counter(sem(f"c_x{b}")) for b in range(B)]
        c_mask = [Counter(sem(f"c_mask{i}")) for i in range(NSTACK)]
        c_store = [Counter(sem(f"c_store{i}")) for i in range(2)]
        c_stack = [Counter(sem(f"c_stack{i}")) for i in range(NSTACK)]
        c_mst = [Counter(sem(f"c_mst{i}")) for i in range(2)]
        c_mld = [Counter(sem(f"c_mld{i}")) for i in range(NSTACK)]
        c_w = Counter(sem("c_w"))
        c_scatter = [Counter(sem(f"c_scatter{i}")) for i in range(2)]
        c_zero = Counter(sem("c_zero"))
        c_xs = [Counter(sem(f"c_xs{i}")) for i in range(3)]
        c_ys = [Counter(sem(f"c_ys{i}")) for i in range(3)]
        NGATHER = 8
        c_gather = [Counter(sem(f"c_gather{i}")) for i in range(NGATHER)]
        c_maskin = Counter(sem("c_maskin"))
        c_out = [Counter(sem(f"c_out{i}")) for i in range(2)]

        scr_qk = nc.dram_tensor("scr_qk", [B, 2, P, PARTS, T], BF16, kind="Internal").ap()
        xs_dram = nc.dram_tensor("xs_dram", [NE * ROWS + FT, E], F32, kind="Internal").ap()
        ys_dram = nc.dram_tensor("ys_dram", [N_TILES * FT, E], F32, kind="Internal").ap()
        scr_m = nc.dram_tensor("scr_m", [B, PARTS * N_HEAD, T], BF16, kind="Internal").ap()

        x_v = x.rearrange("b (q p) e -> b p q e", p=P)
        def load_x(b):
            SP.dma(x_tok[:, b * QT:(b + 1) * QT, :], x_v[b], c_x[b])

        load_x(0)
        for dst, src in ((ident[:, :], ident_in), (wdown_sb[:, :], w_down), (wq_sb[:, :], wq),
                         (swap_sb[:, :], rope_swap), (cos_sb[:, :], rope_cos), (sin_sb[:, :], rope_sin),
                         (wk_sb[:, :], wk_up)):
            SP.dma(dst, src, c_const)
        consts = c_const.all()

        def load_late():
            load_x(1)
            for dst, src in ((wv_sb[:, :], wv_up), (wo_sb[:, :], wo),
                             (nw_rows[:, :],
                              norm_weight.rearrange("(a n) -> a n", a=1).broadcast_to([P, E])),
                             (rw_row[:, :], router_w),
                             (b1_row[0:HT, :], sb1.rearrange("(t p) -> t p", p=P)),
                             (b1_row[HT:, :], eb1.rearrange("e (t p) -> (e t) p", p=P)),
                             (b2_row[0:1, :], sb2.rearrange("(a n) -> a n", a=1)), (b2_row[1:, :], eb2),
                             (before[:, :, :], before_in), (prior[:, :], prior_in),
                             (region[:, :], region_in), (thresholds[:, :, :], thresholds_in),
                             (upto[:, :, :], upto_in), (tile_index[:, :, :], tile_index_in)):
                SP.dma(dst, src, c_late)
            for b in range(2, B):
                load_x(b)

        def load_weights(ffns, after):
            for f in ffns:
                w1, w2 = (sw1, sw2) if f == 0 else (ew1[f - 1], ew2[f - 1])
                SP.dma(w_sb[:, f, 0:H], w1, c_w, after)
                SP.dma(w_sb[:, f, H:W].rearrange("p (t o) -> p t o", o=E),
                       w2.rearrange("(t p) o -> p t o", p=P), c_w)

        stack1 = asb("stack1", [P, S_WORDS])
        stack_mem = [recycled[:, S_WORDS:2 * S_WORDS], stack1[:, :], recycled[:, 0:S_WORDS]]
        q_stack = [m[:, 0:Q_WORDS].bitcast(BF16).rearrange("p (j t) -> p j t", t=T) for m in stack_mem]
        k_stack = [m[:, Q_WORDS:S_WORDS].bitcast(BF16).rearrange("p (h j t) -> p h j t", h=2, t=T)
                   for m in stack_mem]
        v_aug = [asb(f"v_aug{i}", [P, QT, N_HEAD, D + 1]) for i in range(2)]
        probs = asb("probs", [P, NPROB, T])
        mask_f32 = probs[0:N_MASK, 0:2, :]
        mask_bf = probs[0:N_MASK, 2:3, :].bitcast(BF16).rearrange("n a (s t) -> n (a s) t", s=2)
        xT = [asb(f"xT{i}", [P, T]) for i in range(1)]
        latT = [asb(f"latT{i}", [L, T]) for i in range(NSTACK)]
        raw = asb("raw", [P, T])
        turned = asb("turned", [P, T])
        parts = asb("parts", [P, PARTS, T], BF16)
        mx = [asb(f"mx{i}", [P, QT, N_HEAD]) for i in range(2)]
        m_rest = asb("m_rest", [P, QT, N_HEAD])
        m_parts = asb("m_parts", [P, QT, PARTS * N_HEAD], BF16)
        mT = asb("mT", [PARTS * N_HEAD, T], BF16)
        t_mask = SP.dma(mask_f32[:, :, :], mask_rows.rearrange("s n t -> n s t"), c_maskin)
        stack_ready = []

        def clear_stack(i):
            lane = DVE if i < 2 else POOL
            t = lane.do(lambda e: e.memset(stack_mem[i].bitcast(U32), 0), [lane.latest()])
            return lane, t

        def prepare_stack(i, lane, cleared):
            for hp in range(2):
                lane.do(lambda e, i=i, hp=hp: e.memset(
                    k_stack[i][HALF * hp:HALF * hp + PARTS, hp, :, :], 1.0), [cleared])
                r = HALF * hp + ROW_MASK
                for s, stack in ((0, q_stack[i][r:r + N_MASK, :, :]), (1, k_stack[i][r:r + N_MASK, hp, :, :])):
                    src = mask_bf[:, s:s + 1, :].broadcast_to([N_MASK, NP, T])
                    SP.dma(stack, src, c_mask[i], [t_cast, cleared])
            stack_ready.append([c_mask[i].all(), lane.latest()])

        lane, cleared = clear_stack(0)
        t_cast = DVE.do(lambda e: e.tensor_copy(mask_bf[:, :, :], mask_f32[:, :, :]), [t_mask])
        prepare_stack(0, lane, cleared)
        load_late()
        t_zeros = DVE.do(lambda e: e.memset(zeros[:, :, :], 0.0))

        misc_ready = [(n, None) for n in range(len(MISC_BANKS))]

        def misc_take():
            while not misc_ready:
                yield 1
            n, free = misc_ready.pop(0)
            return n, psum[:, MISC_BANKS[n], :], free

        def misc_free(n, token):
            misc_ready.append((n, token))

        state = {k: {} for k in ("stored", "loaded", "m_loaded", "x_done", "m_done", "latT", "v",
                                 "outT", "pv", "filled")}
        def turn_weights():
            n, bank, free = yield from misc_take()
            PE.do(lambda e: e.transpose(bank[:, 0:NE], rw_row[:, :], ident[0:NE, 0:NE]),
                  [free, consts, c_late.all()], False)
            t = PE.do(lambda e: e.transpose(bank[:, P:P + (NE + 1) * HT], b1_row[:, :],
                                            ident[0:(NE + 1) * HT, 0:(NE + 1) * HT]))
            PE.do(lambda e: e.transpose(bank[:, 2 * P:2 * P + NE + 1], b2_row[:, :], ident[0:NE + 1, 0:NE + 1]))
            DVE.do(lambda e: e.tensor_copy(rwT[:, :], bank[:, 0:NE]), [PE.latest()])
            DVE.do(lambda e: e.tensor_copy(b2T[:, :], bank[:, 2 * P:2 * P + NE + 1]))
            state["wT"] = DVE.do(lambda e: e.tensor_copy(b1T[:, :], bank[:, P:P + (NE + 1) * HT]))
            misc_free(n, state["wT"])
            yield

        last = {"rsum": None, "xnT": None, "xT": None, "raw": None, "attn": None, "attnT": None,
                "outT_free": None,
                "latT": [None] * NSTACK, "parts_free": None, "mT_free": None,
                "m_parts_free": None, "mx_free": [None, None]}

        def project(b):
            n, bank, free = yield from misc_take()
            for j in range(QT):
                t = PE.do(lambda e: e.transpose(bank[:, j * P:(j + 1) * P], x_tok[:, b * QT + j, :],
                                                ident[:, :]),
                          [free, c_x[b].all(), consts] if j == 0 else (), j == QT - 1)
            yield 1
            t_xT = ACTE.do(lambda e: e.activation(xT[0][:, :], bank, ACT.Copy), [t, last["xT"]])
            misc_free(n, t_xT)
            yield 2
            n, bank, free = yield from misc_take()
            t = PE.do(lambda e: e.matmul(bank[0:L, :], wdown_sb[:, :], xT[0][:, :], start=True, stop=True),
                      [free, t_xT])
            yield 1
            t_lat = ACTE.do(lambda e: e.activation(latT[b % NSTACK][:, :], bank[0:L, :], ACT.Copy),
                            [t, last["latT"][b % NSTACK]])
            misc_free(n, t_lat)
            state["latT"][b] = t_lat
            for s in range(2):
                w, src = ((wq_sb[:, :], xT[0][:, :]), (wk_sb[:, :], latT[b % NSTACK][:, :]))[s]
                yield 2
                n, bank, free = yield from misc_take()
                t = PE.do(lambda e: e.matmul(bank, w, src, start=True, stop=True), [free, t_lat, t_xT])
                if s == 0:
                    last["xT"] = t
                yield 1
                t_raw = ACTE.do(lambda e: e.activation(raw[:, :], bank, ACT.Copy,
                                                       scale=SCALE if s == 0 else 1.0), [t, last["raw"]])
                misc_free(n, t_raw)
                yield 2
                n, bank, free = yield from misc_take()
                t = PE.do(lambda e: e.matmul(bank, swap_sb[:, :], raw[:, :], start=True, stop=True),
                          [free, t_raw])
                t_c = POOL.do(lambda e: e.tensor_tensor(raw[:, :], raw[:, :], cos_sb[:, :], ALU.mult), [t])
                yield 1
                t_s = DVE.do(lambda e: e.tensor_tensor(turned[:, :], bank, sin_sb[:, :], ALU.mult),
                             [t, last["raw"]])
                misc_free(n, t_s)
                yield 1
                t_r = POOL.do(lambda e: e.tensor_tensor(turned[:, :], turned[:, :], raw[:, :], ALU.add),
                              [t_c, t_s])
                yield 3
                pt = parts
                t_h = ACTE.do(lambda e: e.activation(pt[:, 0, :], turned[:, :], ACT.Copy),
                              [t_r, last["parts_free"]])
                yield 1
                t_r1 = POOL.do(lambda e: e.tensor_tensor(raw[:, :], turned[:, :], pt[:, 0, :],
                                                         ALU.subtract), [t_h])
                yield 3
                t_m = DVE.do(lambda e: e.tensor_copy(pt[:, 1, :], raw[:, :]), [t_r1])
                yield 1
                t_l = POOL.do(lambda e: e.tensor_tensor(pt[:, 2, :], raw[:, :], pt[:, 1, :],
                                                        ALU.subtract), [t_m])
                last["raw"] = t_l
                last["parts_free"] = SP.dma(scr_qk[b, s], pt[:, :, :], c_store[s], [t_l])
            state["stored"][b] = [c_store[0].all(), c_store[1].all()]

        def load_stacks(b):
            i = b % NSTACK
            gate_ = [state["x_done"].get(b - NSTACK)]
            first = gate_ + stack_ready[i] + state["stored"][b] + [t_zeros]
            for hp in range(2):
                SP.dma(q_stack[i][HALF * hp:HALF * hp + PARTS, :, :],
                       zeros[0:PARTS, :, :].rearrange("p j e -> p (j e)").bitcast(BF16).unsqueeze(1)
                       .broadcast_to([PARTS, NP, T]), c_stack[i], first)
            for s in range(2):
                for hp in range(2):
                    src = scr_qk[b, s].rearrange("(j h d) c t -> h c d j t", h=2, d=D)[hp]
                    for n, term in enumerate(TERMS):
                        r = HALF * hp + ROW_TERM + D * n
                        dst = (q_stack[i][r:r + D, :, :] if s == 0 else k_stack[i][r:r + D, hp, :, :])
                        SP.dma(dst, src[term[s]], c_stack[i], first)
            state["loaded"][b] = [c_stack[i].all()]

        def values(b):
            n, bank, free = yield from misc_take()
            for j in range(QT):
                t = PE.do(lambda e, j=j: e.matmul(bank[:, j * P:(j + 1) * P], latT[b % NSTACK][:, j * P:(j + 1) * P],
                                                  wv_sb[:, :], start=True, stop=True),
                          [free, state["latT"][b]] if j == 0 else (), j == QT - 1)
            last["latT"][b % NSTACK] = t
            yield 1
            t_v = ACTE.do(lambda e: e.activation(
                v_aug[b % 2][:, :, :, 0:D], bank.rearrange("p (q h d) -> p q h d", q=QT, d=D), ACT.Copy),
                [t, v_free[b % 2]])
            misc_free(n, t_v)
            state["v"][b] = t_v

        def place_maxima(b):
            m = mx[b % 2]
            neg = m_parts
            part = lambda c: neg[:, :, c * N_HEAD:(c + 1) * N_HEAD]
            t1 = DVE.do(lambda e: e.tensor_scalar(part(0), m[:, :, :], -1.0, None, ALU.mult),
                        [state["m_done"][b], last["m_parts_free"]])
            t2 = DVE.do(lambda e: e.scalar_tensor_tensor(out=m_rest[:, :, :], in0=m[:, :, :], scalar=-1.0,
                                                         in1=part(0), op0=ALU.mult, op1=ALU.subtract), [t1])
            last["mx_free"][b % 2] = t2
            t3 = DVE.do(lambda e: e.tensor_copy(part(1), m_rest[:, :, :]), [t2])
            t4 = DVE.do(lambda e: e.tensor_tensor(part(2), m_rest[:, :, :], part(1), ALU.subtract), [t3])
            yield 3
            n, bank, free = yield from misc_take()
            bank_bf = bank.bitcast(BF16)
            for j in range(QT):
                t = PE.do(lambda e, j=j: e.transpose(bank_bf[0:PARTS * N_HEAD, j * P:(j + 1) * P],
                                                     neg[:, j, :], ident_bf[:, :]),
                          [free, t4, t_identb] if j == 0 else (), j == QT - 1)
            last["m_parts_free"] = t
            t5 = ACTE.do(lambda e: e.activation(mT[:, :], bank_bf[0:PARTS * N_HEAD, 0:T], ACT.Copy),
                         [t, last["mT_free"]])
            misc_free(n, t5)
            t6 = SP.dma(scr_m[b], mT[:, :], c_mst[b % 2], [t5])
            last["mT_free"] = t6
            for hp in range(2):
                SP.dma(q_stack[b % NSTACK][HALF * hp:HALF * hp + PARTS, :, :],
                       scr_m[b].rearrange("(c j h) t -> h c j t", c=PARTS, h=2)[hp],
                       c_mld[b % NSTACK], [t6, state["m_done"][b]])
            state["m_loaded"][b] = c_mld[b % NSTACK].all()
            yield

        def finish(b):
            tiles = slice(b * QT, (b + 1) * QT)
            attn_row = attn[:, :, :].rearrange("p q (h d) -> p q h d", d=D)
            yield 2
            for j in range(QT):
                n, bank, free = yield from misc_take()
                for g in range(NG):
                    t = PE.do(lambda e: e.transpose(
                        bank[:, g * P:(g + 1) * P], outT[0][:, g, j * P:(j + 1) * P], ident[:, :]),
                        [free, state["outT"][b]] if g == 0 else (), g == NG - 1)
                yield 1
                heads = bank.rearrange("p (h c) -> p h c", c=VW)
                t_rs = DVE.do(lambda e: e.reciprocal(rsum[:, :], heads[:, :, D]),
                              [t, last["rsum"]])
                t_a = DVE.do(lambda e: e.tensor_tensor(
                    attn_row[:, j, :, :], heads[:, :, 0:D],
                    rsum[:, :].unsqueeze(2).broadcast_to([P, N_HEAD, D]), ALU.mult), [t_rs, last["attn"]])
                last["rsum"] = t_a
                misc_free(n, t_a)
            last["outT_free"] = t
            yield 1
            n, bank, free = yield from misc_take()
            for j in range(QT):
                t = PE.do(lambda e: e.transpose(bank[:, j * P:(j + 1) * P], attn[:, j, :], ident[:, :]),
                          [free, t_a] if j == 0 else (), j == QT - 1)
            last["attn"] = t
            yield 1
            t_aT = ACTE.do(lambda e: e.activation(attnT[:, :], bank, ACT.Copy), [t, last["attnT"]])
            misc_free(n, t_aT)
            yield 2
            n, bank, free = yield from misc_take()
            for j in range(QT):
                t = PE.do(lambda e: e.matmul(bank[:, j * P:(j + 1) * P], attnT[:, j * P:(j + 1) * P],
                                             wo_sb[:, :], start=True, stop=True),
                          [free, t_aT] if j == 0 else (), j == QT - 1)
            last["attnT"] = t
            yield 1
            rows = x_tok[:, tiles, :]
            t_y = DVE.do(lambda e: e.tensor_tensor(rows, bank.rearrange("p (q e) -> p q e", q=QT), rows,
                                                   ALU.add), [t])
            misc_free(n, t_y)
            yield 1
            for j in range(QT):
                t_s = DVE.do(lambda e: e.bn_stats(stats[:, j, :], x_tok[:, b * QT + j, :]), [t_y])
                if j % 2:
                    yield 1
            for j in range(QT):
                t_m = DVE.do(lambda e: e.bn_aggr(moments[:, j, :], stats[:, j, :]), [t_s])
            var = moments[:, :, 1]
            yield 2
            POOL.do(lambda e: e.tensor_scalar(rstd[:, :], var, LN_EPS, None, ALU.add), [t_m])
            POOL.do(lambda e: e.tensor_tensor(rstd[:, :], rstd[:, :], minus_half[:, :], ALU.pow), [t_half])
            POOL.do(lambda e: e.tensor_tensor(rms[:, :], rstd[:, :], rstd[:, :], ALU.mult))
            POOL.do(lambda e: e.tensor_tensor(rms[:, :], rms[:, :], var, ALU.mult))
            POOL.do(lambda e: e.tensor_scalar(rms[:, :], rms[:, :], RMS_EPS, None, ALU.add))
            t2 = POOL.do(lambda e: e.tensor_tensor(rms[:, :], rms[:, :], minus_half[:, :], ALU.pow))
            yield 6
            for j in range(QT):
                t_n = DVE.do(lambda e: e.tensor_scalar(
                    x_tok[:, b * QT + j, :], x_tok[:, b * QT + j, :], moments[:, j, 0:1], rstd[:, j:j + 1],
                    ALU.subtract, ALU.mult), [t2], j == QT - 1)
                if j % 2:
                    yield 1
            for j in range(QT):
                t_xn = DVE.do(lambda e: e.scalar_tensor_tensor(
                    out=xn[b % 2][:, j, :], in0=x_tok[:, b * QT + j, :], scalar=rms[:, j:j + 1],
                    in1=nw_rows[:, :], op0=ALU.mult, op1=ALU.mult),
                    [t_n, c_scatter[b % 2].all() if b >= 2 else None], j == QT - 1)
                if j % 2:
                    yield 1 + j // 2
            n, bank, free = yield from misc_take()
            for j in range(QT):
                t = PE.do(lambda e: e.transpose(bank[:, j * P:(j + 1) * P], xn[b % 2][:, j, :], ident[:, :]),
                          [free, t_xn] if j == 0 else (), j == QT - 1)
            flat = lambda a: a[:, tiles, :].rearrange("p q t -> p (q t)")
            yield 1
            t_xnT = ACTE.do(lambda e: e.activation(xnT[:, :], bank, ACT.Copy), [t, last["xnT"]])
            t_hi = ACTE.do(lambda e: e.activation(flat(xnT_hi), bank, ACT.Copy))
            misc_free(n, t_hi)
            yield 2
            POOL.do(lambda e: e.tensor_tensor(flat(xnT_lo), xnT[:, :], flat(xnT_hi).bitcast(F32),
                                              ALU.subtract), [t_hi])
            n, bank, free = yield from misc_take()
            for j in range(QT):
                t = PE.do(lambda e: e.matmul(bank[:, j * NE:(j + 1) * NE], xnT[:, j * P:(j + 1) * P],
                                             rwT[:, :], start=True, stop=True),
                          [free, t_xnT, state["wT"]] if j == 0 else (), j == QT - 1)
            last["xnT"] = POOL.latest()
            yield 1
            t_e = ACTE.do(lambda e: e.activation(gate[:, :, :].rearrange("p q n -> p (q n)"),
                                                 bank[:, 0:QT * NE], ACT.Exp, scale=-1.0), [t])
            misc_free(n, t_e)
            yield 2
            t1 = DVE.do(lambda e: e.tensor_scalar(gate[:, :, :], gate[:, :, :], 1.0, None, ALU.add), [t_e])
            t2 = DVE.do(lambda e: e.reciprocal(gate[:, :, :], gate[:, :, :]), [t1])
            mine = gate[:, :, :].unsqueeze(3).broadcast_to([P, QT, NE, NE])
            other = gate[:, :, :].unsqueeze(2).broadcast_to([P, QT, NE, NE])
            earlier = before[:, :, :].unsqueeze(1).broadcast_to([P, QT, NE, NE])
            t3 = DVE.do(lambda e: e.tensor_tensor(above[:, :, :, :], other, mine, ALU.is_gt), [t2])
            t4 = DVE.do(lambda e: e.tensor_tensor(equal[:, :, :, :], other, mine, ALU.is_equal))
            yield 1
            t5 = DVE.do(lambda e: e.tensor_tensor(equal[:, :, :, :], equal[:, :, :, :], earlier, ALU.mult), [t4])
            t6 = DVE.do(lambda e: e.tensor_tensor(above[:, :, :, :], above[:, :, :, :], equal[:, :, :, :],
                                                  ALU.add), [t5])
            yield 1
            t7 = DVE.do(lambda e: e.tensor_reduce(rank[:, :, :], above[:, :, :, :], AXIS_X, ALU.add), [t6])
            t8 = DVE.do(lambda e: e.tensor_scalar(chosen[:, :, :], rank[:, :, :], float(TOPK), None,
                                                  ALU.is_lt), [t7])
            yield 3
            n, bank, free = yield from misc_take()
            sel = chosen[:, :, :].rearrange("p q n -> p (q n)")
            PE.do(lambda e: e.matmul(bank[:, 0:QT * NE], prior[:, :], sel, start=True, stop=True),
                  [free, t8], False)
            t = PE.do(lambda e: e.matmul(bank[:, P:P + QT * NE], ones[:, :], sel, start=True, stop=True))
            ahead = bank[:, 0:QT * NE].rearrange("p (q n) -> p q n", n=NE)
            total = bank[:, P:P + QT * NE].rearrange("p (q n) -> p q n", n=NE)
            for k in range(TOPK):
                tw = DVE.do(lambda e: e.scalar_tensor_tensor(
                    out=picked[:, k, :, :], in0=rank[:, :, :], scalar=float(k), in1=gate[:, :, :],
                    op0=ALU.is_equal, op1=ALU.mult), [t7])
            tw = DVE.do(lambda e: e.tensor_reduce(share[:, :, tiles], picked[:, 0:TOPK, :, :], AXIS_X,
                                                  ALU.add), [tw])
            yield 1
            tg = DVE.do(lambda e: e.tensor_tensor(gsum[:, :], share[:, 0, tiles], share[:, 1, tiles],
                                                  ALU.add), [tw])
            tg = DVE.do(lambda e: e.tensor_scalar(gsum[:, :], gsum[:, :], TOPK_EPS, None, ALU.add), [tg])
            tg = DVE.do(lambda e: e.reciprocal(gsum[:, :], gsum[:, :]), [tg])
            DVE.do(lambda e: e.tensor_tensor(share[:, :, tiles], share[:, :, tiles],
                                             gsum[:, :].unsqueeze(1).broadcast_to([P, TOPK, QT]),
                                             ALU.mult), [tg])
            yield 1
            for j in range(QT):
                ta = DVE.do(lambda e: e.tensor_tensor(row_all[:, j, :], ahead[:, j, :], filled[:, :],
                                                      ALU.add), [t, t_filled, state["filled"].get(0)])
                state["filled"][0] = DVE.do(lambda e: e.tensor_tensor(
                    filled[:, :], total[:, j, :], filled[:, :], ALU.add), [ta])
            misc_free(n, state["filled"][0])
            yield 1
            for k in range(TOPK):
                tr = DVE.do(lambda e: e.scalar_tensor_tensor(
                    out=picked[:, TOPK + k, :, :], in0=rank[:, :, :], scalar=float(k),
                    in1=row_all[:, :, :], op0=ALU.is_equal, op1=ALU.mult), [ta])
            tr = DVE.do(lambda e: e.tensor_reduce(row_f[:, :, :], picked[:, TOPK:, :, :], AXIS_X,
                                                  ALU.add), [tr])
            tr = DVE.do(lambda e: e.tensor_copy(row_of[:, :, tiles], row_f[:, :, :]), [tr])
            yield 1
            start(scatter(b, tr))

        def scatter(b, tr):
            for j in range(QT):
                for k in range(TOPK):
                    POOL.wait([tr])
                    c = c_scatter[b % 2]
                    c.count += 16
                    nc.gpsimd.indirect_dma_start(
                        xs_dram, bass.IndirectOffsetOnAxis(row_of[:, k, b * QT + j:b * QT + j + 1], 0),
                        xn[b % 2][:, j, :], None).then_inc(c.sem, 16)
                    yield 2

        ring = {"exp": 0, "max": 0}
        exp_free = [None] * len(EXP_BANKS)
        max_free = [None] * len(MAX_BANKS)
        probs_free = [None] * NPROB
        exp_tok = {}

        def exp_slot(G, s):
            b, g = divmod(G, NG)
            qs, ks = q_stack[b % NSTACK], k_stack[b % NSTACK]
            r = ring["exp"] % len(EXP_BANKS)
            ring["exp"] += 1
            bank = psum[:, EXP_BANKS[r], :]
            if s < GH:
                plan = [(g * GH + s, 0, 0)]
            elif s < 2 * GH:
                plan = [(g * GH + s - GH, 1, 0), (g * GH + s - GH, 3, 3 * P)]
            else:
                plan = [(g * GH + 2 * (s - 2 * GH) + i, 2, 2 * P * i) for i in range(2)]
            for n, (h, kt, at) in enumerate(plan):
                j, hp = divmod(h, 2)
                width = T - kt * P
                t = PE.do(lambda e, j=j, hp=hp, kt=kt, at=at, width=width: e.matmul(
                    bank[:, at:at + width], ks[:, hp, j, kt * P:(kt + 1) * P], qs[:, j, kt * P:T],
                    start=True, stop=True),
                    [exp_free[r], state["m_loaded"][b]] if n == 0 else (), n == len(plan) - 1)
            if s == SLOTS - 1 and g == NG - 1:
                state["x_done"][b] = t
            held = (G * SLOTS + s) % NPROB
            te = ACTE.do(lambda e: e.activation(probs[:, held, :], bank, ACT.Exp),
                         [t, probs_free[held]])
            exp_free[r] = te
            exp_tok[G, s] = te

        def pv(G, kt):
            b, g = divmod(G, NG)
            at = {0: (0, 0), 1: (GH, 0), 3: (GH, 3 * P)}
            need = [exp_tok[G, {0: GH - 1, 1: 2 * GH - 1, 3: 2 * GH - 1, 2: SLOTS - 1}[kt]]]
            if kt == 0:
                need += [pv_free[0], state["v"][b]]
            for i in range(GH):
                h = g * GH + i
                width = T - kt * P
                s, c = (2 * GH + i // 2, 2 * P * (i % 2)) if kt == 2 else (at[kt][0] + i, at[kt][1])
                t = PE.do(lambda e, i=i, h=h, s=s, c=c, width=width: e.matmul(
                    psum[VW * i:VW * i + D + 1, PV_BANK, kt * P:T], v_aug[b % 2][:, kt, h, :],
                    probs[:, (G * SLOTS + s) % NPROB, c:c + width], start=(kt == 0), stop=(kt == 2),
                    skip_group_check=True, tile_position=(0, VW * i)), need if i == 0 else (), i == GH - 1)
            done = {0: range(GH), 1: (), 3: range(GH, 2 * GH), 2: range(2 * GH, SLOTS)}[kt]
            for s in done:
                probs_free[(G * SLOTS + s) % NPROB] = t
            if kt == 2:
                state["pv"][G] = t
                if g == NG - 1:
                    v_free[b % 2] = t

        def pv_out(G):
            b, g = divmod(G, NG)
            t = ACTE.do(lambda e: e.activation(outT[0][:, g, :], psum[:, PV_BANK, :], ACT.Copy),
                        [state["pv"][G], last["outT_free"]])
            pv_free[0] = t
            state["outT"][b] = t

        def max_slot(G, s):
            b, g = divmod(G, NG)
            qs, ks = q_stack[b % NSTACK], k_stack[b % NSTACK]
            r = ring["max"] % len(MAX_BANKS)
            ring["max"] += 1
            bank = psum[:, MAX_BANKS[r], :]
            if s < GH:
                plan = [(g * GH + s, 3, 0)]
            elif s < 2 * GH:
                plan = [(g * GH + s - GH, 2, 0), (g * GH + s - GH, 0, 3 * P)]
            else:
                plan = [(g * GH + 2 * (s - 2 * GH) + i, 1, 2 * P * i) for i in range(2)]
            for n, (h, qt, at) in enumerate(plan):
                j, hp = divmod(h, 2)
                width = (qt + 1) * P
                t = PE.do(lambda e, j=j, hp=hp, qt=qt, at=at, width=width: e.matmul(
                    bank[:, at:at + width], qs[:, j, qt * P:(qt + 1) * P], ks[:, hp, j, 0:width],
                    start=True, stop=True),
                    [max_free[r]] + state["loaded"][b] if n == 0 else (), n == len(plan) - 1)
            m = mx[b % 2]
            need = [t, last["mx_free"][b % 2]]
            if s < 2 * GH:
                for h, qt, at in plan:
                    width = (qt + 1) * P
                    t = DVE.do(lambda e, h=h, qt=qt, at=at, width=width: e.tensor_reduce(
                        m[:, qt, h:h + 1], bank[:, at:at + width], AXIS_X, ALU.max), need)
            else:
                h = plan[0][0]
                t = DVE.do(lambda e: e.tensor_reduce(
                    m[:, 1, h:h + 2], bank.rearrange("p (h k) -> p h k", h=2), AXIS_X, ALU.max), need)
            max_free[r] = t
            if s == SLOTS - 1 and g == NG - 1:
                state["m_done"][b] = t

        background, clock, STEPS = [], [0], 3

        def advance():
            clock[0] += 1
            steps = 0
            for job in list(background):
                if job[1] > clock[0] or steps == STEPS:
                    continue
                steps += 1
                wait = next(job[0], None)
                if wait is None:
                    background.remove(job)
                else:
                    job[1] = clock[0] + wait

        def start(work, first=False):
            job = [work, clock[0]]
            background.insert(0 if first else len(background), job)
            return job

        def complete(job):
            while job in background:
                advance()

        def run_all():
            while background:
                advance()

        start(project(0))
        run_all()
        load_stacks(0)
        prepare_stack(1, *clear_stack(1))
        t_identb = DVE.do(lambda e: e.tensor_copy(ident_bf[:, :], ident[:, :]), [consts])
        for v in range(2):
            t_v1 = DVE.do(lambda e: e.memset(v_aug[v][:, :, :, D:D + 1], 1.0))
        v_free = [t_v1, t_v1]
        DVE.do(lambda e: e.memset(ones[:, :], 1.0))
        pv_free = [DVE.do(lambda e: e.memset(psum[:, PV_BANK, :], 0.0))]
        t_half = DVE.do(lambda e: e.memset(minus_half[:, :], -0.5))
        t_filled = DVE.do(lambda e: e.tensor_copy(filled[:, :], region[:, :]), [c_late.all()])
        start(turn_weights())
        jobs = {}
        for idx in range(-LEAD, B * NG + 1):
            X, M = idx, idx + LEAD
            b, g = divmod(idx, NG)
            if g == 2 and 0 <= b + 1 < B:
                jobs["maxima", b + 1] = start(place_maxima(b + 1), first=True)
                advance()
            if g == 3 and 0 <= b + 1 < B:
                jobs["values", b + 1] = start(values(b + 1))
            if g == 0 and 0 < b + 2 < B:
                complete(jobs["project", b + 2])
                load_stacks(b + 2)
            if g == 0 and b - 1 == B - NSTACK:
                load_weights(range(FIRST_FFNS), [state["x_done"][b - 1]])
            if g == 0 and b - 1 == B - NSTACK + 1:
                load_weights(range(FIRST_FFNS, NE + 1), [state["x_done"][b - 1]])
            if idx == -LEAD:
                jobs["project", 1] = start(project(1))
            if idx == 1 - LEAD:
                prepare_stack(2, *clear_stack(2))
            if g == 0 and 2 < b + 3 < B or idx == -3:
                jobs["project", max(b + 3, 2)] = start(project(max(b + 3, 2)))
            for s in range(SLOTS):
                if 0 <= X < B * NG:
                    if s == 0 and g == 0:
                        complete(jobs["maxima", b])
                        complete(jobs["values", b])
                    exp_slot(X, s)
                if 0 <= M < B * NG:
                    max_slot(M, s)
                if s == 6 and 0 <= X < B * NG:
                    pv(X, 0)
                if s == 9 and 0 <= X < B * NG:
                    pv(X, 1)
                if s == 0 and 1 <= X <= B * NG:
                    pv(X - 1, 3)
                if s == 1 and 1 <= X <= B * NG:
                    pv(X - 1, 2)
                if s == 3 and 1 <= X <= B * NG:
                    pv_out(X - 1)
                    if g == 0:
                        if b > 1:
                            complete(jobs["finish", b - 2])
                        jobs["finish", b - 1] = start(finish(b - 1))
                advance()

        att_end = [ln.latest() for ln in (PE, ACTE, DVE, POOL)]
        att.close()

        def fsb(name, shape, dt=F32, side="left"):
            return ctx.enter_context(nc.sbuf_tensor(name, shape, dt, side=side))

        w_split = fsb("w_split", [P, NE + 1, 2, 2, H], F32R)
        x_in = [fsb(f"x_in{i}", [P, 2, E]) for i in range(3)]
        y_out = [fsb(f"y_out{i}", [P, 2, E]) for i in range(3)]
        n_tiles = fsb("n_tiles", [P, NE])
        over = fsb("over", [P, NE, MAX_E_TILES])
        cum_all = fsb("cum_all", [P, NE, NE])
        cum = fsb("cum", [P, NE])
        passed, passed_n = (a[:, 0:N_TILES * NE].rearrange("p (t n) -> p t n", n=NE) for a in (xnT, attnT))
        t_expert = fsb("t_expert", [P, N_TILES])
        t_before = fsb("t_before", [P, N_TILES])
        t_row = fsb("t_row", [P, N_TILES])
        table = fsb("table", [P, 2, N_TILES], U32)
        delta = fsb("delta", [P, NE])
        step_ = fsb("step", [P, NE])
        shift = fsb("shift", [P, TOPK * NT])
        row_y = fsb("row_y", [P, TOPK, NT], U32)
        inside = attn[:, :, :].rearrange("p q (a n) -> p (q a) n", n=NE)
        region_end = fsb("region_end", [P, NE], U32)
        f_stats = fsb("f_stats", [P, 2, 6])
        f_moments = [fsb(f"f_moments{i}", [P, 2, 2]) for i in range(4)]
        f_rstd = [fsb(f"f_rstd{i}", [P, 4]) for i in range(2)]

        split_done = {}

        def split_weights():
            weights = c_w.all()
            for f in list(range(1, NE + 1)) + [0]:
                raw_w = w_sb[:, f, :].rearrange("p (w h) -> p w h", w=2)
                th = ACTE.do(lambda e: e.activation(w_split[:, f, :, 0, :], raw_w, ACT.Copy),
                             [weights] + att_end)
                yield 1
                split_done[f] = DVE.do(lambda e: e.tensor_tensor(
                    w_split[:, f, :, 1, :], raw_w, w_split[:, f, :, 0, :].bitcast(F32), ALU.subtract),
                    [th] + att_end)
                yield 2

        start(split_weights())
        run_all()

        t = DVE.do(lambda e: e.tensor_copy(region_end[:, :], filled[:, :]),
                   [ln.latest() for ln in (PE, ACTE, DVE, POOL)])
        t_end = t
        t = DVE.do(lambda e: e.tensor_tensor(cum[:, :], filled[:, :], region[:, :], ALU.subtract))
        t = DVE.do(lambda e: e.tensor_tensor(over[:, :, :], cum[:, :].unsqueeze(2).broadcast_to(
            [P, NE, MAX_E_TILES]), thresholds[:, :, :], ALU.is_gt), [t])
        t = DVE.do(lambda e: e.tensor_reduce(n_tiles[:, :], over[:, :, :], AXIS_X, ALU.add), [t])
        t = DVE.do(lambda e: e.tensor_tensor(cum_all[:, :, :], n_tiles[:, :].unsqueeze(1).broadcast_to(
            [P, NE, NE]), upto[:, :, :], ALU.mult), [t])
        t = DVE.do(lambda e: e.tensor_reduce(cum[:, :], cum_all[:, :, :], AXIS_X, ALU.add), [t])
        per_tile = lambda a: a[:, :].unsqueeze(1).broadcast_to([P, N_TILES, NE])
        t = DVE.do(lambda e: e.tensor_tensor(passed[:, :, :], tile_index[:, :, :], per_tile(cum),
                                             ALU.is_ge), [t])
        t = DVE.do(lambda e: e.tensor_tensor(passed_n[:, :, :], passed[:, :, :], per_tile(n_tiles),
                                             ALU.mult), [t])
        t = DVE.do(lambda e: e.tensor_reduce(t_before[:, :], passed_n[:, :, :], AXIS_X, ALU.add), [t])
        t = DVE.do(lambda e: e.tensor_reduce(t_expert[:, :], passed[:, :, :], AXIS_X, ALU.add), [t])
        t = DVE.do(lambda e: e.tensor_tensor(t_before[:, :], tile_index[:, :, 0], t_before[:, :],
                                             ALU.subtract), [t])
        t = DVE.do(lambda e: e.tensor_scalar(t_row[:, :], t_expert[:, :], float(ROWS), None, ALU.mult), [t])
        t = DVE.do(lambda e: e.scalar_tensor_tensor(out=t_row[:, :], in0=t_before[:, :], scalar=float(FT),
                                                    in1=t_row[:, :], op0=ALU.mult, op1=ALU.add), [t])
        DVE.do(lambda e: e.tensor_scalar(table[:, 0, :], t_expert[:, :], float(NE - 1), None, ALU.min), [t])
        t_table = DVE.do(lambda e: e.tensor_scalar(table[:, 1, :], t_row[:, :], float(NE * ROWS), None,
                                                   ALU.min), [t])

        t = DVE.do(lambda e: e.tensor_tensor(delta[:, :], cum[:, :], n_tiles[:, :], ALU.subtract), [t])
        t = DVE.do(lambda e: e.scalar_tensor_tensor(out=delta[:, :], in0=delta[:, :], scalar=float(FT),
                                                    in1=region[:, :], op0=ALU.mult, op1=ALU.subtract), [t])
        t = DVE.do(lambda e: e.tensor_copy(step_[:, :], delta[:, :]), [t])
        t = DVE.do(lambda e: e.tensor_tensor(step_[:, 1:], delta[:, 1:], delta[:, 0:NE - 1],
                                             ALU.subtract), [t])
        rows_x = row_of[:, :, :].rearrange("p k t -> p (k t)")
        each = lambda a: a[:, :].unsqueeze(1).broadcast_to([P, TOPK * NT, NE])
        t = DVE.do(lambda e: e.tensor_tensor(inside, rows_x.unsqueeze(2).broadcast_to([P, TOPK * NT, NE]),
                                             each(region), ALU.is_ge), [t])
        t = DVE.do(lambda e: e.tensor_tensor(inside, inside, each(step_), ALU.mult), [t])
        t = DVE.do(lambda e: e.tensor_reduce(shift[:, :], inside, AXIS_X, ALU.add), [t])
        t_row_y = DVE.do(lambda e: e.tensor_tensor(row_y[:, :, :].rearrange("p k t -> p (k t)"), rows_x,
                                                   shift[:, :], ALU.add), [t])

        rows_of = lambda dram, first: dram[bass.ds(first, FT), :].rearrange("(j p) e -> p j e", p=P)
        SP.dma(rows_of(xs_dram, NE * ROWS), zeros[:, :, :], c_zero, [t_zeros])
        SP.wait([t_end])
        for e_ in range(NE):
            first = nc.sync.value_load(region_end[0:1, e_:e_ + 1], min_val=0, max_val=NE * ROWS - FT)
            SP.dma(rows_of(xs_dram, first), zeros[:, :, :], c_zero)
        xs_ready = [c_zero.all()] + [c.all() for c in c_scatter]
        ffn_free = [ln.latest() for ln in (PE, ACTE, DVE, POOL)]
        rec.close()

        g_f = [fsb(f"g_f{i}", [P, HT, FT], side="right") for i in range(2)]
        g_hi = [fsb(f"g_hi{i}", [P, HT, FT], F32R, side="right") for i in range(2)]
        g_lo = [fsb(f"g_lo{i}", [P, HT, FT], F32R, side="right") for i in range(2)]
        x_hi = [fsb(f"x_hi{i}", [P, FT], F32R, side="right") for i in range(2)]
        x_lo = [fsb(f"x_lo{i}", [P, FT], F32R, side="right") for i in range(2)]
        yT = [fsb(f"yT{i}", [P, FT], side="right") for i in range(2)]
        w1_cur = [fsb(f"w1_cur{i}", [P, 2, H], F32R, side="right") for i in range(2)]
        w2_cur = [fsb(f"w2_cur{i}", [P, 2, H], F32R, side="right") for i in range(2)]
        gathered = [outT[0][:, i // 2, (i % 2) * FT:(i % 2 + 1) * FT].rearrange("p (k e) -> p k e", k=TOPK)
                    for i in range(NGATHER)]
        IN_BANKS, HID_BANKS, OUT_BANKS = (0, 1), (2, 3, 4, 5), (6, 7)
        N_SHARED = NT // 2
        N_UNITS = N_TILES + N_SHARED
        unit = [dict() for _ in range(N_UNITS)]

        def bank_of(ring_, n):
            return psum[:, ring_[n % len(ring_)], :]

        def tok(u, name):
            return unit[u].get(name) if 0 <= u < N_UNITS else None

        def fetch(u):
            SP.wait([t_table])
            row = nc.sync.value_load(table[0:1, 1, u:u + 1], min_val=0, max_val=NE * ROWS)
            unit[u]["x_in"] = SP.dma(x_in[u % 3][:, :, :], rows_of(xs_dram, row), c_xs[u % 3],
                                     xs_ready + ffn_free + [tok(u - 3, "turned")])

        def turn_in(u):
            bank = bank_of(IN_BANKS, u)
            for j in range(2):
                t = PE.do(lambda e: e.transpose(bank[:, j * P:(j + 1) * P], x_in[u % 3][:, j, :], ident[:, :]),
                          [unit[u]["x_in"], tok(u - 2, "x_lo")] + ffn_free if j == 0 else (), j == 1)
            unit[u]["turned"] = t
            unit[u]["x_hi"] = ACTE.do(lambda e: e.activation(x_hi[u % 2][:, :], bank[:, 0:FT], ACT.Copy),
                                      [t, tok(u - 2, "hid")])

        def split_in(u):
            unit[u]["x_lo"] = DVE.do(lambda e: e.tensor_tensor(
                x_lo[u % 2][:, :], bank_of(IN_BANKS, u)[:, 0:FT], x_hi[u % 2][:, :].bitcast(F32),
                ALU.subtract), [unit[u]["x_hi"], tok(u - 2, "hid")])

        def take_w1(u):
            DVE.wait([t_table] + ffn_free)
            e_ = nc.vector.value_load(table[0:1, 0, u:u + 1], min_val=0, max_val=NE - 1)
            unit[u]["e_dve"] = e_
            unit[u]["w1"] = DVE.do(lambda e: e.tensor_copy(
                w1_cur[u % 2][:, :, :], w_split[:, bass.ds(e_ + 1, 1), 0, :, :].squeeze(1)),
                [tok(u - 2, "hid")] + list(split_done.values()))

        def take_w2(u):
            e_ = unit[u]["e_dve"]
            unit[u]["w2"] = DVE.do(lambda e: e.tensor_copy(
                w2_cur[u % 2][:, :, :], w_split[:, bass.ds(e_ + 1, 1), 1, :, :].squeeze(1)),
                [tok(u - 2, "out")])

        def hidden(u):
            routed = u < N_TILES
            if routed:
                xh, xl, w = x_hi[u % 2][:, :], x_lo[u % 2][:, :], w1_cur[u % 2]
                need = [unit[u]["x_lo"], unit[u]["w1"]]
            else:
                two = slice(2 * (u - N_TILES), 2 * (u - N_TILES) + 2)
                xh = xnT_hi[:, two, :].rearrange("p q t -> p (q t)")
                xl = xnT_lo[:, two, :].rearrange("p q t -> p (q t)")
                w = w_split[:, 0, 0, :, :]
                need = ffn_free + [split_done[0]]
            for i in range(2):
                bank = bank_of(HID_BANKS, 2 * u + i)
                for c in range(2):
                    t4 = 2 * i + c
                    at = slice(t4 * P, (t4 + 1) * P)
                    dst = bank[:, c * FT:(c + 1) * FT]
                    for n, (wp, xp) in enumerate(((0, xh), (0, xl), (1, xh))):
                        t = PE.do(lambda e: e.matmul(dst, w[:, wp, at], xp, start=(n == 0), stop=(n == 2)),
                                  need + [tok(u - 2, f"g{i}")] if c == 0 and n == 0 else (),
                                  c == 1 and n == 2)
                unit[u][f"hid{i}"] = t
            unit[u]["hid"] = t

        def act(u):
            routed = u < N_TILES
            if routed:
                ACTE.wait([t_table])
                e_ = nc.scalar.value_load(table[0:1, 0, u:u + 1], min_val=0, max_val=NE - 1)
                unit[u]["e_act"] = e_
            for t4 in range(HT):
                i, c = divmod(t4, 2)
                bank = bank_of(HID_BANKS, 2 * u + i)
                bias = b1T[:, bass.ds((e_ + 1) * HT + t4, 1)] if routed else b1T[:, t4:t4 + 1]
                t = ACTE.do(lambda e: e.activation(g_f[u % 2][:, t4, :], bank[:, c * FT:(c + 1) * FT],
                                                   ACT.Relu, bias=bias),
                            [unit[u][f"hid{i}"], tok(u - 2, "g_lo")] if c == 0 else (), c == 1)
                if c == 1:
                    unit[u][f"g{i}"] = t

        def split_act(u):
            routed = u < N_TILES
            th = DVE.do(lambda e: e.tensor_copy(g_hi[u % 2][:, :, :], g_f[u % 2][:, :, :]),
                        [unit[u]["g1"], tok(u - 2, "out")])
            lane = POOL if routed else DVE
            unit[u]["g_lo"] = lane.do(lambda e: e.tensor_tensor(
                g_lo[u % 2][:, :, :], g_f[u % 2][:, :, :], g_hi[u % 2][:, :, :].bitcast(F32),
                ALU.subtract), [th, tok(u - 2, "out")])

        def project_out(u):
            routed = u < N_TILES
            bank = bank_of(OUT_BANKS, u)
            w = w2_cur[u % 2] if routed else w_split[:, 0, 1, :, :]
            need = [unit[u]["g_lo"], unit[u].get("w2"), tok(u - 2, "y")]
            n = 0
            for t4 in range(HT):
                at = slice(t4 * P, (t4 + 1) * P)
                for wp, g in ((0, g_hi), (0, g_lo), (1, g_hi)):
                    t = PE.do(lambda e: e.matmul(bank[:, 0:FT], w[:, wp, at], g[u % 2][:, t4, :],
                                                 start=(n == 0), stop=(n == 3 * HT - 1)),
                              need if n == 0 else (), n == 3 * HT - 1)
                    n += 1
            unit[u]["out"] = t
            bias = b2T[:, bass.ds(unit[u]["e_act"] + 1, 1)] if routed else b2T[:, 0:1]
            unit[u]["yT"] = ACTE.do(lambda e: e.activation(yT[u % 2][:, :], bank[:, 0:FT], ACT.Identity,
                                                           bias=bias), [t, tok(u - 2, "y_turned")])

        def turn_out(u):
            routed = u < N_TILES
            bank = bank_of(OUT_BANKS, u)
            for j in range(2):
                t = PE.do(lambda e: e.transpose(bank[:, FT + j * P:FT + (j + 1) * P],
                                                yT[u % 2][:, j * P:(j + 1) * P], ident[:, :]),
                          [unit[u]["yT"]] if j == 0 else (), j == 1)
            unit[u]["y_turned"] = t
            y = bank[:, FT:2 * FT].rearrange("p (j e) -> p j e", j=2)
            if routed:
                unit[u]["y"] = DVE.do(lambda e: e.tensor_copy(y_out[u % 3][:, :, :], y),
                                      [t, tok(u - 3, "stored")])
                unit[u]["stored"] = SP.dma(rows_of(ys_dram, u * FT), y_out[u % 3][:, :, :], c_ys[u % 3],
                                           [unit[u]["y"]])
            else:
                pair = slice(2 * (u - N_TILES), 2 * (u - N_TILES) + 2)
                unit[u]["y"] = DVE.do(lambda e: e.tensor_tensor(x_tok[:, pair, :], y, x_tok[:, pair, :],
                                                                ALU.add), [t])

        gather_done = {}
        gather_free = [None] * NGATHER
        t_rstd = {}

        def gather(i):
            n = i % NGATHER
            POOL.wait([t_row_y, gather_free[n]] + [c.all() for c in c_ys])
            for k in range(TOPK):
                c_gather[n].count += 16
                nc.gpsimd.indirect_dma_start(
                    gathered[n][:, k, :], None, ys_dram,
                    bass.IndirectOffsetOnAxis(row_y[:, k, i:i + 1], 0)).then_inc(c_gather[n].sem, 16)
            gather_done[i] = c_gather[n].all()

        def combine(m):
            for i in (2 * m, 2 * m + 1):
                for k in range(TOPK):
                    t = DVE.do(lambda e: e.scalar_tensor_tensor(
                        out=x_tok[:, i, :], in0=gathered[i % NGATHER][:, k, :],
                        scalar=share[:, k, i:i + 1], in1=x_tok[:, i, :], op0=ALU.mult, op1=ALU.add),
                        [gather_done[i], unit[N_TILES + m]["y"]] if k == 0 else [t])
                gather_free[i % NGATHER] = t
                if i + NGATHER < NT:
                    gather(i + NGATHER)
                t = DVE.do(lambda e: e.bn_stats(f_stats[:, i % 2, :], x_tok[:, i, :]), [t])
                t = DVE.do(lambda e: e.bn_aggr(f_moments[m % 4][:, i % 2, :], f_stats[:, i % 2, :]), [t])
            both = f_rstd[m // 2 % 2]
            t = DVE.do(lambda e: e.tensor_scalar(both[:, m % 2 * 2:m % 2 * 2 + 2], f_moments[m % 4][:, :, 1],
                                                 LN_EPS, None, ALU.add), [t])
            if m % 2:
                t_rstd[m // 2] = POOL.do(lambda e: e.tensor_tensor(
                    both[:, :], both[:, :], minus_half[:, 0:4], ALU.pow), [t, t_half])

        def write_out(m):
            for i in (2 * m, 2 * m + 1):
                at = 2 * (m % 2) + i % 2
                t = DVE.do(lambda e: e.tensor_scalar(
                    x_tok[:, i, :], x_tok[:, i, :], f_moments[m % 4][:, i % 2, 0:1],
                    f_rstd[m // 2 % 2][:, at:at + 1], ALU.subtract, ALU.mult), [t_rstd[m // 2]])
            SP.dma(out.rearrange("b (q p) e -> p (b q) e", p=P)[:, 2 * m:2 * m + 2, :],
                   x_tok[:, 2 * m:2 * m + 2, :], c_out[0], [t])

        for u in range(3):
            fetch(u)
        for i in range(-1, N_UNITS + 7):
            if 3 <= i + 3 < N_TILES:
                fetch(i + 3)
            if 0 <= i + 1 < N_TILES:
                turn_in(i + 1)
                take_w1(i + 1)
            if 0 <= i < N_UNITS:
                hidden(i)
                act(i)
            if 0 <= i - 1 < N_UNITS:
                split_act(i - 1)
            if 0 <= i + 1 < N_TILES:
                split_in(i + 1)
            if 0 <= i - 3 < N_UNITS:
                turn_out(i - 3)
            if 0 <= i - 2 < N_UNITS:
                project_out(i - 2)
            if 0 <= i - 1 < N_TILES:
                take_w2(i - 1)
            if i - 3 == N_TILES - 1:
                for n in range(NGATHER):
                    gather(n)
            if 0 <= i - 4 - N_TILES < N_SHARED:
                combine(i - 4 - N_TILES)
            if 0 <= i - 6 - N_TILES < N_SHARED:
                write_out(i - 6 - N_TILES)
        SP.wait([c.all() for c in c_out + c_ys])


_INS = ["L0_attn_x", "L0_attn_wq", "L0_attn_w_down", "L0_attn_wk_up", "L0_attn_wv_up", "L0_attn_wo",
        "L0_ffn_norm_weight", "L0_ffn_router_w", "L0_ffn_sw1", "L0_ffn_sb1", "L0_ffn_sw2", "L0_ffn_sb2",
        "L0_ffn_ew1", "L0_ffn_eb1", "L0_ffn_ew2", "L0_ffn_eb2"]


def shape_constants(T, E, n_expert, n_token):
    D = E // N_HEAD
    inv = 1.0 / ROPE_THETA ** (np.arange(0, D, 2, dtype=np.float32) / D)
    ang = np.outer(np.arange(T, dtype=np.float32), inv)
    cos, sin = np.cos(ang).astype(np.float32), np.sin(ang).astype(np.float32)
    pair = (np.arange(E) % D) // 2
    sign = np.where(np.arange(E) % 2 == 0, -1.0, 1.0).astype(np.float32)
    rope_cos = np.ascontiguousarray(cos[:, pair].T)
    rope_sin = np.ascontiguousarray((sin[:, pair] * sign).T)
    swap = np.zeros((E, E), np.float32)
    swap[np.arange(E) ^ 1, np.arange(E)] = 1.0
    t = np.arange(T)
    mask_q, mask_k = [], []
    for tile in range(T // P):
        for page in range(1, P // PAGE):
            start = tile * P
            mask_q.append(np.where((t >= start) & (t < start + page * PAGE), MASK_BIG, 0.0))
            mask_k.append(((t >= start + page * PAGE) & (t < start + (page + 1) * PAGE)) * 1.0)
    mask = np.stack([np.stack(mask_q), np.stack(mask_k)]).astype(np.float32)
    e = np.arange(n_expert)
    n_rows = n_token + 2 * P
    wide = lambda a: np.ascontiguousarray(np.broadcast_to(a.astype(np.float32), (P,) + a.shape))
    prior = np.triu(np.ones((P, P), np.float32), 1)
    n_tiles = n_token * TOPK // (2 * P) + n_expert - 1
    thresholds = np.broadcast_to(2 * P * np.arange(n_token // (2 * P)), (n_expert, n_token // (2 * P)))
    tile_index = np.broadcast_to(np.arange(n_tiles)[:, None], (n_tiles, n_expert))
    return [rope_cos, rope_sin, swap, mask, np.eye(P, dtype=np.float32), wide(e[None, :] < e[:, None]),
            prior, wide(e * n_rows), wide(thresholds), wide(e[None, :] <= e[:, None]), wide(tile_index)]


def kernel(**inputs):
    import numpy as _np
    import concourse.bacc as _bacc
    from concourse import mybir as _mybir
    from concourse.bass_utils import run_bass_kernel_spmd as _run

    nc = _bacc.Bacc("TRN2", target_bir_lowering=False, num_devices=1)
    arrays, args = {}, []

    def give(name, a):
        a = _np.ascontiguousarray(a)
        arrays[name] = a
        args.append(nc.dram_tensor(name, a.shape, _mybir.dt.from_np(a.dtype), kind="ExternalInput").ap())

    for name in _INS:
        give(f"in_{name}", inputs[name])
    B, T, E = inputs["L0_attn_x"].shape
    for i, a in enumerate(shape_constants(T, E, inputs["L0_ffn_ew1"].shape[0], B * T)):
        give(f"const_{i}", a)
    args.append(nc.dram_tensor("out", (B, T, E), F32, kind="ExternalOutput").ap())
    build(nc, *args)
    r = _run(nc, [arrays], core_ids=[0])
    return r.results[0]["out"]
```
